# Optimizing a Trainium2 kernel written in Bass

```python
import numpy as np
import jax
import jax.numpy as jnp

def _softmax(x, axis=-1):
    return jax.nn.softmax(x, axis=axis)

def _gelu(x):
    return jax.nn.gelu(x, approximate=True)

def _silu(x):
    return jax.nn.silu(x)

def _sigmoid(x):
    return jax.nn.sigmoid(x)

def _layernorm(x, axis=-1, eps=1e-05):
    m = jnp.mean(x, axis=axis, keepdims=True)
    v = jnp.var(x, axis=axis, keepdims=True)
    return (x - m) / jnp.sqrt(v + eps)

def _scatter_add(tgt, idx, src, axis=0):
    return tgt.at[idx].add(src)

def _segment_sum(src, seg, n):
    return jax.ops.segment_sum(src, seg, n)
kernel_name = 'mk_macaron_d1_jaxref_r8_658e68'

def setup_inputs(seed: int=0):
    np.random.seed(seed)
    _w = jnp.asarray

    def _L0_attn_setup():
        import jax, jax.numpy as jnp
        import numpy as np
        D_MODEL = 128
        N_HEADS = 16
        HEAD_DIM = D_MODEL // N_HEADS
        SCALE = HEAD_DIM ** (-0.5)

        def apply_rotary(x):
            seq_len = x.shape[-2]
            freqs = 10000.0 ** (jnp.arange(0, HEAD_DIM, 2.0, dtype=jnp.float32) / HEAD_DIM)
            t = jnp.arange(seq_len, dtype=jnp.float32)
            angles = t[:, None] * freqs[None, :]
            sin = jnp.sin(angles)[None, None]
            cos = jnp.cos(angles)[None, None]
            x1, x2 = (x[..., ::2], x[..., 1::2])
            return jnp.concatenate([x1 * cos - x2 * sin, x2 * cos + x1 * sin], axis=-1)
        key = jax.random.key(seed)
        ks = jax.random.split(key, 5)
        B, T = (2, 256)
        std = D_MODEL ** (-0.5)
        return {'x': jax.random.normal(ks[0], (B, T, D_MODEL), dtype=jnp.float32), 'qkv_w': jax.random.normal(ks[1], (D_MODEL, 3 * D_MODEL), dtype=jnp.float32) * std, 'qkv_b': jnp.zeros((3 * D_MODEL,), dtype=jnp.float32), 'out_w': jax.random.normal(ks[2], (D_MODEL, D_MODEL), dtype=jnp.float32) * std, 'out_b': jnp.zeros((D_MODEL,), dtype=jnp.float32)}
    _L0_attn_in = _L0_attn_setup()

    def _L0_ffn_setup():
        import jax, jax.numpy as jnp
        import numpy as np
        B, T, C = (4, 256, 128)
        E, F, K = (8, 256, 2)
        key = jax.random.key(seed)
        k0, k1, k2, k3 = jax.random.split(key, 4)
        s = lambda d: 1.0 / np.sqrt(d)
        x = jax.random.normal(k0, (B, T, C), dtype=jnp.float32)
        Wr = jax.random.normal(k1, (E, C), dtype=jnp.float32) * s(C)
        W1 = jax.random.normal(k2, (E, 2 * F, C), dtype=jnp.float32) * s(C)
        W2 = jax.random.normal(k3, (E, C, F), dtype=jnp.float32) * s(F)
        return {'x': x, 'Wr': Wr, 'W1': W1, 'W2': W2}
    _L0_ffn_in = _L0_ffn_setup()
    _d = {'L0_attn_x': _L0_attn_in['x'], 'L0_attn_qkv_w': _L0_attn_in['qkv_w'], 'L0_attn_qkv_b': _L0_attn_in['qkv_b'], 'L0_attn_out_w': _L0_attn_in['out_w'], 'L0_attn_out_b': _L0_attn_in['out_b'], 'L0_ffn_Wr': _L0_ffn_in['Wr'], 'L0_ffn_W1': _L0_ffn_in['W1'], 'L0_ffn_W2': _L0_ffn_in['W2']}
    _x0 = _d['L0_attn_x']
    _d['L0_attn_x'] = jax.random.normal(jax.random.fold_in(jax.random.key(seed), 1), (4, 1024, 128), dtype=_x0.dtype)
    del _x0
    return _d

def reference(L0_attn_x, L0_attn_qkv_w, L0_attn_qkv_b, L0_attn_out_w, L0_attn_out_b, L0_ffn_Wr, L0_ffn_W1, L0_ffn_W2):

    def _L0_attn_ref(x, qkv_w, qkv_b, out_w, out_b):
        import jax, jax.numpy as jnp
        import numpy as np
        D_MODEL = 128
        N_HEADS = 16
        HEAD_DIM = D_MODEL // N_HEADS
        SCALE = HEAD_DIM ** (-0.5)

        def apply_rotary(x):
            seq_len = x.shape[-2]
            freqs = 10000.0 ** (jnp.arange(0, HEAD_DIM, 2.0, dtype=jnp.float32) / HEAD_DIM)
            t = jnp.arange(seq_len, dtype=jnp.float32)
            angles = t[:, None] * freqs[None, :]
            sin = jnp.sin(angles)[None, None]
            cos = jnp.cos(angles)[None, None]
            x1, x2 = (x[..., ::2], x[..., 1::2])
            return jnp.concatenate([x1 * cos - x2 * sin, x2 * cos + x1 * sin], axis=-1)
        B, T, D = x.shape
        qkv = x @ qkv_w + qkv_b
        q, k, v = jnp.split(qkv, 3, axis=-1)

        def to_heads(a):
            return a.reshape(B, T, N_HEADS, HEAD_DIM).transpose(0, 2, 1, 3)
        q, k, v = (to_heads(q), to_heads(k), to_heads(v))
        q = apply_rotary(q)
        k = apply_rotary(k)
        scores = jnp.einsum('bhqd,bhkd->bhqk', q, k) * SCALE
        weights = jax.nn.softmax(scores, axis=-1)
        attn = jnp.einsum('bhqk,bhkd->bhqd', weights, v)
        attn = attn.transpose(0, 2, 1, 3).reshape(B, T, D)
        return attn @ out_w + out_b

    def _L0_ffn_ref(x, Wr, W1, W2):
        import jax, jax.numpy as jnp
        import numpy as np
        B, T, C = (4, 256, 128)
        E, F, K = (8, 256, 2)
        Bb, Tt, Cc = x.shape
        flat = x.reshape(-1, Cc)
        N = flat.shape[0]
        logits = flat @ Wr.T
        weights, ids = jax.lax.top_k(logits, K)
        weights = jax.nn.softmax(weights, axis=-1)
        rows = jnp.arange(N)[:, None]
        router_weights = jnp.zeros((N, E), dtype=flat.dtype).at[rows, ids].add(weights)
        h = jnp.einsum('nc,efc->nef', flat, W1)
        val, gate = (h[..., :F], h[..., F:])
        act = val * jax.nn.silu(gate)
        expert_outputs = jnp.einsum('nef,ecf->nec', act, W2)
        out = jnp.einsum('nec,ne->nc', expert_outputs, router_weights)
        return out.reshape(Bb, Tt, Cc)
    x = L0_attn_x
    x = x + 0.5 * _L0_ffn_ref(_layernorm(x, axis=-1), L0_ffn_Wr, L0_ffn_W1, L0_ffn_W2)
    x = x + _L0_attn_ref(_layernorm(x, axis=-1), L0_attn_qkv_w, L0_attn_qkv_b, L0_attn_out_w, L0_attn_out_b)
    x = x + 0.5 * _L0_ffn_ref(_layernorm(x, axis=-1), L0_ffn_Wr, L0_ffn_W1, L0_ffn_W2)
    return x

_drawn_inputs = setup_inputs


def setup_inputs(seed=0):
    import zlib

    import numpy as np

    out = dict(_drawn_inputs(seed))
    spreads = {'L0_attn_qkv_b': (0.0, 0.1), 'L0_attn_out_b': (0.0, 0.1)}
    factors = {}
    for name, (base, spread) in spreads.items():
        noise = np.random.default_rng([zlib.crc32(name.encode()), seed]).standard_normal(out[name].shape)
        drawn = base * np.exp(spread * noise) if base else spread * noise
        out[name] = jnp.asarray(drawn.astype(out[name].dtype))
    for name, factor in factors.items():
        out[name] = (out[name] * factor).astype(out[name].dtype)
    return out
```

```python
from contextlib import ExitStack

import numpy as np

import concourse.bass as bass
from concourse import mybir

F32 = mybir.dt.float32
BF16 = mybir.dt.bfloat16
U32 = mybir.dt.uint32
I32 = mybir.dt.int32
ALU = mybir.AluOpType
ACT = mybir.ActivationFunctionType
AX_X = mybir.AxisListType.X

P = 128
B, T, D = 4, 1024, 128
H, HD = 16, 8
E, F = 8, 256
N = B * T
EPS = 1e-5
SCALE = float(HD) ** -0.5
CH = 512
TPC = CH // P
NCH = N // CH
CPB = T // CH
NH = B * H
KB = T // P
PARTS = 3
STACK = PARTS * PARTS * HD
FILLED = 96
ROWS = FILLED + PARTS
QG = T // 4
VW = 32
QSLOTS = 4
PSLOTS = 4
NEWTON = 4


def at_least(eng, sem, count):
    if isinstance(count, int) and count <= 0:
        return
    eng.wait_ge(sem, count)


class Order:

    def __init__(self, eng, sem):
        self.eng, self.sem, self.base, self.k = eng, sem, 0, 0

    def start(self, base):
        self.base, self.k = base, 0

    def mark(self, ins):
        self.k += 1
        ins.then_inc(self.sem, 1)

    def wait(self):
        self.eng.wait_ge(self.sem, self.base + self.k)

    def then(self, ins):
        self.mark(ins)
        self.wait()


def steps(eng, count, per, body):
    rounds = count // per
    for u in range(per):
        body(0, u)
    with eng.Fori(1, rounds - 1) as r:
        for u in range(per):
            body(r, u)
    for u in range(per):
        body(rounds - 1, u)


def build(nc, x_in, qkv_w, qkv_b, v_b, out_w, out_b, wr_t, w1_t, w2_t, cos_t, sin_t, out):
    q_stack = nc.dram_tensor("q_stack", (NH, PARTS, HD, T), BF16).ap()
    k_stack = nc.dram_tensor("k_stack", (NH, PARTS, HD, T), BF16).ap()
    o_parts = nc.dram_tensor("o_parts", (NH, P, QG), F32).ap()
    with ExitStack() as ctx:
        def sb(name, shape, dt=F32):
            return ctx.enter_context(nc.sbuf_tensor(name, shape, dt))

        def sem(name):
            return ctx.enter_context(nc.semaphore(name))

        w1 = sb("w1", [P, E, 2 * F])
        w2 = sb("w2", [P, E, F // P, D])
        wr = sb("wr", [P, E])
        wqkv = sb("wqkv", [P, 5, D])
        bqk = sb("bqk", [P, 4])
        bv = sb("bv", [P, D])
        wo = sb("wo", [P, D])
        bo = sb("bo", [P, D])
        cos = sb("cos", [P, T])
        sin = sb("sin", [P, T])
        ident = sb("ident", [P, P])
        identb = sb("identb", [P, P], BF16)
        expert_id = sb("expert_id", [P, E])
        X = sb("X", [P, N // P, D])
        V = sb("V", [P, B, H, KB, HD])
        stats = sb("stats", [P, TPC, 6])
        mv = sb("mv", [P, TPC, 2])
        var = sb("var", [P, TPC])
        half_var = sb("half_var", [P, TPC])
        rstd = sb("rstd", [P, TPC])
        tmp = sb("tmp", [P, TPC])
        xn = sb("xn", [P, 2, TPC, D])
        xnT = sb("xnT", [P, 2, CH])
        logits = sb("logits", [P, TPC, E])
        top = sb("top", [P, TPC, 8])
        top_id = sb("top_id", [P, TPC, 8], U32)
        top_idf = sb("top_idf", [P, TPC, 2])
        gap = sb("gap", [P, TPC])
        tanh_gap = sb("tanh_gap", [P, TPC])
        wt = sb("wt", [P, 2, TPC])
        pick = sb("pick", [P, 2, TPC, E])
        rw = sb("rw", [P, 2, TPC, E])
        sg = sb("sg", [P, 2, CH])
        act = sb("act", [P, 2, 2, CH])
        rot = sb("rot", [P, 2, 2, CH])
        qf = sb("qf", [P, 2, CH])
        rest = sb("rest", [P, 2, CH])
        parts = sb("parts", [P, 2, PARTS, CH], BF16)
        Q = sb("Q", [P, QSLOTS, T], BF16)
        K = sb("K", [P, QSLOTS, T], BF16)
        probs = sb("probs", [P, PSLOTS, T])
        vh = sb("vh", [P, 2, KB, VW])
        mx = sb("mx", [P, 2, 2, KB])
        negm = sb("negm", [P, 2, KB])
        mparts = sb("mparts", [P, 2, PARTS, KB], BF16)
        mrow = sb("mrow", [PARTS * KB, 2, P], BF16)
        ot = sb("ot", [P, 2, QG])
        att = sb("att", [P, CH])
        den = sb("den", [P, CH])
        rden = sb("rden", [P, CH])
        attn = sb("attn", [P, CH])

        ps = ctx.enter_context(nc.psum_tensor("ps", [P, 8, 512], F32))
        hid = [ps[:, 0, :], ps[:, 1, :], ps[:, 2, :], ps[:, 3, :]]
        ypsum = [ps[:, 4 + s, :].rearrange("p (t c) -> p t c", t=TPC) for s in range(2)]
        tpsum = ps[:, 6, :]
        rpsum = ps[:, 7, 0:TPC * E].rearrange("p (t e) -> p t e", t=TPC)
        score = [ps[:, 2 * s:2 * s + 2, :] for s in range(2)]
        maxps = [ps[:, 4 + s, :] for s in range(2)]
        opsum = [ps[:, 6 + s, 0:QG] for s in range(2)]
        mpsum = [ps[0:PARTS * KB, 6 + s, 0:P // 2].bitcast(BF16) for s in range(2)]

        w_loaded = sem("w_loaded")
        x_loaded = sem("x_loaded")
        consts_ready = sem("consts_ready")
        pool_order = sem("pool_order")
        norm_order = sem("norm_order")
        route_order = sem("route_order")
        xn_ready = sem("xn_ready")
        xT_in_psum = sem("xT_in_psum")
        xnT_ready = sem("xnT_ready")
        xnT_used = sem("xnT_used")
        logits_in_psum = sem("logits_in_psum")
        gap_ready = sem("gap_ready")
        tanh_ready = sem("tanh_ready")
        route_ready = sem("route_ready")
        gate_in_psum = sem("gate_in_psum")
        value_in_psum = sem("value_in_psum")
        silu_done = sem("silu_done")
        act_ready = sem("act_ready")
        y_in_psum = sem("y_in_psum")
        acc_done = sem("acc_done")
        qkv_in_psum = sem("qkv_in_psum")
        qkv_read = sem("qkv_read")
        rot_ready = sem("rot_ready")
        rot_sum = sem("rot_sum")
        hi_ready = sem("hi_ready")
        rest_ready = sem("rest_ready")
        mid_ready = sem("mid_ready")
        lo_ready = sem("lo_ready")
        stored = [sem("q_stored"), sem("k_stored")]
        head_loaded = [sem(f"head_loaded{u}") for u in range(QSLOTS)]
        max_in_psum = sem("max_in_psum")
        max_read = sem("max_read")
        max_ready = sem("max_ready")
        mparts_ready = sem("mparts_ready")
        mT_in_psum = sem("mT_in_psum")
        mrow_ready = sem("mrow_ready")
        mrow_loaded = [sem(f"mrow_loaded{u}") for u in range(QSLOTS)]
        vh_ready = sem("vh_ready")
        scores_in_psum = sem("scores_in_psum")
        probs_ready = sem("probs_ready")
        probs_used = sem("probs_used")
        ot_ready = sem("ot_ready")
        ot_stored = [sem(f"ot_stored{s}") for s in range(2)]
        att_loaded = sem("att_loaded")
        attn_ready = sem("attn_ready")
        proj_in_psum = sem("proj_in_psum")
        waits_passed = sem("waits_passed")
        out_stored = sem("out_stored")
        add_order = sem("add_order")
        bias_added = sem("bias_added")

        def alone(eng):
            eng.sem_inc(waits_passed, 1)

        block = ctx.enter_context(nc.Block())

        @block.sync
        def _(sp):
            for c in range(NCH):
                sp.dma_start(X[:, TPC * c:TPC * (c + 1), :],
                             x_in[CH * c:CH * (c + 1), :].rearrange("(t p) d -> p t d", p=P)).then_inc(x_loaded, 16)
                if c == 0:
                    sp.dma_start(wr[:], wr_t).then_inc(w_loaded, 16)
                    sp.dma_start(w1[:], w1_t).then_inc(w_loaded, 16)
                    sp.dma_start(w2[:], w2_t).then_inc(w_loaded, 16)
            sp.dma_start(wqkv[:], qkv_w).then_inc(w_loaded, 16)
            sp.dma_start(bqk[:], qkv_b).then_inc(w_loaded, 16)
            sp.dma_start(bv[:], v_b.to_broadcast((P, D))).then_inc(w_loaded, 16)
            sp.dma_start(wo[:], out_w).then_inc(w_loaded, 16)
            sp.dma_start(bo[:], out_b.to_broadcast((P, D))).then_inc(w_loaded, 16)
            sp.dma_start(cos[:], cos_t).then_inc(w_loaded, 16)
            sp.dma_start(sin[:], sin_t).then_inc(w_loaded, 16)

            def store_parts(r, u):
                for w, stack in ((0, q_stack), (1, k_stack)):
                    sp.wait_ge(lo_ready, 4 * r + 2 * u + w + 1)
                    for i in range(PARTS):
                        dst = stack[bass.ds(r * H, H), i, :, u * CH:(u + 1) * CH]
                        sp.dma_start(dst, parts[:, w, i, :]).then_inc(stored[w], 16)

            steps(sp, NCH, CPB, store_parts)
            for w in range(2):
                sp.wait_ge(stored[w], 16 * PARTS * NCH)

            def load_head(r, u):
                n = QSLOTS * r + u
                at_least(sp, probs_used, KB * (n - QSLOTS + 1))
                q_part = q_stack[bass.ds(n, 1)].rearrange("n i d t -> n (i d) t").to_broadcast((PARTS, PARTS * HD, T))
                sp.dma_start(Q[0:STACK, u, :], q_part).then_inc(head_loaded[u], 16)
                for j in range(PARTS):
                    at = j * PARTS * HD
                    sp.dma_start(K[at:at + PARTS * HD, u, :],
                                 k_stack[bass.ds(n, 1), j, :, :].to_broadcast((PARTS, HD, T))).then_inc(head_loaded[u], 16)

            def load_mrow(r, u):
                n = QSLOTS * r + u
                sp.wait_ge(mrow_ready, n + 1)
                sp.dma_start(Q[FILLED:ROWS, u, :].rearrange("p (t c) -> p t c", t=KB),
                             mrow[:, u % 2, :]).then_inc(mrow_loaded[u], 16)

            def store_o(r, u):
                n = QSLOTS * r + u
                sp.wait_ge(ot_ready, n + 1)
                sp.dma_start(o_parts[bass.ds(n, 1)].rearrange("n p q -> (n p) q"), ot[:, u % 2, :]).then_inc(ot_stored[u % 2], 16)

            def later(r, u, by):
                return r + (u + by) // QSLOTS, (u + by) % QSLOTS

            sp.wait_ge(consts_ready, 3)
            load_head(0, 0)
            load_head(0, 1)
            load_head(0, 2)
            load_mrow(0, 0)

            def head(r, u, load=True, rows=True):
                if load:
                    load_head(*later(r, u, 3))
                if not (isinstance(r, int) and r == 0 and u == 0):
                    store_o(*later(r, u, -1))
                if rows:
                    load_mrow(*later(r, u, 1))

            for u in range(QSLOTS):
                head(0, u)
            with sp.Fori(1, NH // QSLOTS - 1) as r:
                for u in range(QSLOTS):
                    head(r, u)
            last = NH // QSLOTS - 1
            for u in range(QSLOTS):
                head(last, u, load=u < 1, rows=u < 3)
            store_o(last, QSLOTS - 1)
            for s in range(2):
                sp.wait_ge(ot_stored[s], 16 * NH // 2)

            def load_att(r, u):
                c = CPB * r + u
                at_least(sp, proj_in_psum, c)
                for g in range(2):
                    src = o_parts[bass.ds(r * H, H)]
                    at = 32 * (2 * u + g)
                    sp.dma_start(att[:, g * QG:(g + 1) * QG], src[:, at:at + HD, :]).then_inc(att_loaded, 16)
                    sp.dma_start(den[:, g * QG:(g + 1) * QG], src[:, at + HD:at + 2 * HD, :]).then_inc(att_loaded, 16)

            def store_out(c):
                sp.wait_ge(acc_done, E * (NCH + c + 1))
                row = c * CH
                sp.dma_start(out[bass.ds(row, CH), :].rearrange("(t p) d -> p t d", p=P),
                             X[:, bass.ds(c * TPC, TPC), :]).then_inc(out_stored, 16)

            load_att(0, 0)
            load_att(0, 1)

            def tail(r, u):
                load_att(*((r + 1, u)))
                store_out(CPB * r + u)

            with sp.Fori(0, NCH // CPB - 1) as r:
                for u in range(CPB):
                    tail(r, u)
            for u in range(CPB):
                store_out(NCH - CPB + u)
            sp.wait_ge(out_stored, 16 * NCH)

        @block.gpsimd
        def _(pool):
            seq = Order(pool, pool_order)
            seq.then(nc.gpsimd.memset(ident[:], 0.0))
            seq.then(nc.gpsimd.affine_select(out=ident[:], in_=ident[:], compare_op=ALU.not_equal, fill=1.0,
                                             base=0, pattern=[[-1, P]], channel_multiplier=1))
            nc.gpsimd.tensor_copy(identb[:], ident[:]).then_inc(consts_ready, 1)
            for e in range(E):
                seq.mark(nc.gpsimd.memset(expert_id[:, e:e + 1], float(e)))
            seq.then(nc.gpsimd.memset(vh[:], 1.0))
            seq.then(nc.gpsimd.memset(Q[64:96, :, :], 0.0))
            seq.then(nc.gpsimd.memset(K[64:96, :, :], 0.0))
            nc.gpsimd.memset(K[96:P, :, :], 1.0).then_inc(consts_ready, 2)

            def split(r, u):
                for w in range(2):
                    z = 4 * r + 2 * u + w
                    pool.wait_ge(rot_ready, z + 1)
                    at_least(pool, mid_ready, z - 1)
                    nc.gpsimd.tensor_tensor(qf[:, w, :], rot[:, w, 0, :], rot[:, w, 1, :], ALU.add).then_inc(rot_sum, 1)
                    pool.wait_ge(rot_sum, z + 1)
                    pool.wait_ge(hi_ready, z + 1)
                    nc.gpsimd.tensor_tensor(rest[:, w, :], qf[:, w, :], parts[:, w, 0, :], ALU.subtract).then_inc(rest_ready, 1)
                    pool.wait_ge(rest_ready, z + 1)
                    pool.wait_ge(mid_ready, z + 1)
                    nc.gpsimd.tensor_tensor(parts[:, w, 2, :], rest[:, w, :], parts[:, w, 1, :], ALU.subtract).then_inc(lo_ready, 1)

            steps(pool, NCH, CPB, split)

            PER = 4
            order0 = seq.base + seq.k

            def max_parts(r, u):
                n = QSLOTS * r + u
                s = u % 2
                seq.start(PER * n + order0)
                pool.wait_ge(max_ready, n + 1)
                at_least(pool, mT_in_psum, n - 1)
                alone(pool)
                seq.then(nc.gpsimd.tensor_scalar(negm[:, 0, :], mx[:, s, 0, :], -1.0, None, ALU.mult))
                alone(pool)
                seq.then(nc.gpsimd.tensor_copy(mparts[:, s, 0, :], negm[:, 0, :]))
                seq.then(nc.gpsimd.tensor_tensor(negm[:, 1, :], negm[:, 0, :], mparts[:, s, 0, :], ALU.subtract))
                alone(pool)
                seq.then(nc.gpsimd.tensor_copy(mparts[:, s, 1, :], negm[:, 1, :]))
                nc.gpsimd.tensor_tensor(mparts[:, s, 2, :], negm[:, 1, :], mparts[:, s, 1, :], ALU.subtract).then_inc(mparts_ready, 1)

            def v_head(r, u):
                n = QSLOTS * r + u
                at_least(pool, probs_used, KB * (n - 1))
                alone(pool)
                nc.gpsimd.tensor_copy(vh[:, u % 2, :, 0:HD],
                                      V[:].rearrange("p b h k d -> p (b h) k d")[:, bass.ds(n, 1), :, :]
                                      .rearrange("p n k d -> p (n k) d")).then_inc(vh_ready, 1)

            pool.wait_ge(qkv_read, 3 * NCH)
            pool.wait_ge(consts_ready, 3)

            def head(r, u):
                v_head(r, u)
                max_parts(r, u)

            steps(pool, NH, QSLOTS, head)

        @block.scalar
        def _(sc):
            def xT_copy(p, k):
                sc.wait_ge(xT_in_psum, p + 1)
                at_least(sc, xnT_used, p - 1)
                nc.scalar.activation(xnT[:, k, :], tpsum, ACT.Copy).then_inc(xnT_ready, 1)

            def tanh_of_gap(f):
                sc.wait_ge(gap_ready, f + 1)
                nc.scalar.activation(tanh_gap[:], gap[:], ACT.Tanh, scale=0.5).then_inc(tanh_ready, 1)

            def ffn_chunk(f, p, k, more):
                for e in range(E):
                    for j in range(2):
                        a = 2 * (E * f + e) + j
                        sc.wait_ge(gate_in_psum, a + 1)
                        at_least(sc, act_ready, a - 1)
                        nc.scalar.activation(sg[:, j, :], hid[2 * j], ACT.Silu).then_inc(silu_done, 1)
                    if more and e == 3:
                        xT_copy(p + 1, 1 - k)
                    if more and e == 5:
                        tanh_of_gap(f + 1)

            def ffn(f0, p0):
                rounds = NCH // CPB
                xT_copy(p0, 0)
                tanh_of_gap(f0)
                for u in range(CPB):
                    ffn_chunk(f0 + u, p0 + u, u, True)
                with sc.Fori(1, rounds - 1) as r:
                    for u in range(CPB):
                        ffn_chunk(f0 + CPB * r + u, p0 + CPB * r + u, u, True)
                for u in range(CPB):
                    ffn_chunk(f0 + NCH - CPB + u, p0 + NCH - CPB + u, u, u < CPB - 1)

            ffn(0, 0)

            def qkv_chunk(r, u):
                xT_copy(NCH + CPB * r + u, u)
                for w in range(2):
                    z = 4 * r + 2 * u + w
                    sc.wait_ge(rot_sum, z + 1)
                    at_least(sc, stored[w], 16 * PARTS * (CPB * r + u))
                    nc.scalar.activation(parts[:, w, 0, :], qf[:, w, :], ACT.Copy).then_inc(hi_ready, 1)
                    sc.wait_ge(rest_ready, z + 1)
                    nc.scalar.activation(parts[:, w, 1, :], rest[:, w, :], ACT.Copy).then_inc(mid_ready, 1)

            steps(sc, NCH, CPB, qkv_chunk)

            def mrow_copy(r, u):
                n = QSLOTS * r + u
                sc.wait_ge(mT_in_psum, n + 1)
                if not (isinstance(r, int) and r == 0 and u < 2):
                    back = (u - 2) % QSLOTS
                    sc.wait_ge(mrow_loaded[back], 16 * (r + (1 if u >= 2 else 0)))
                nc.scalar.activation(mrow[:, u % 2, :], mpsum[u % 2], ACT.Copy).then_inc(mrow_ready, 1)

            def o_copy(r, u):
                n = QSLOTS * r + u
                sc.wait_ge(probs_used, KB * (n + 1))
                if not (isinstance(r, int) and r == 0 and u < 2):
                    sc.wait_ge(ot_stored[u % 2], 16 * (2 * r + u // 2))
                nc.scalar.activation(ot[:, u % 2, :], opsum[u % 2], ACT.Copy).then_inc(ot_ready, 1)

            def head(r, u, more=True, first=False):
                n = QSLOTS * r + u
                for kb in range(KB):
                    g = KB * n + kb
                    sc.wait_ge(scores_in_psum, g + 1)
                    at_least(sc, probs_used, g - PSLOTS + 1)
                    nc.scalar.activation(probs[:, kb % PSLOTS, :], score[kb % 2].rearrange("p a b -> p (a b)"),
                                         ACT.Exp, scale=SCALE).then_inc(probs_ready, 1)
                    if kb == 2 and not first:
                        o_copy(r + (u - 1) // QSLOTS, (u - 1) % QSLOTS)
                    if kb == 4 and more:
                        mrow_copy(r + (u + 1) // QSLOTS, (u + 1) % QSLOTS)

            mrow_copy(0, 0)
            for u in range(QSLOTS):
                head(0, u, first=(u == 0))
            with sc.Fori(1, NH // QSLOTS - 1) as r:
                for u in range(QSLOTS):
                    head(r, u)
            for u in range(QSLOTS):
                head(NH // QSLOTS - 1, u, more=u < QSLOTS - 1)
            o_copy(NH // QSLOTS - 1, QSLOTS - 1)

            ffn(NCH, 2 * NCH)

        @block.tensor
        def _(pe):
            def x_transposes(p, k):
                pe.wait_ge(xn_ready, p + 1)
                at_least(pe, xnT_ready, p)
                for t in range(TPC):
                    last = nc.tensor.transpose(tpsum[:, t * P:(t + 1) * P], xn[:, k, t, :], ident[:])
                last.then_inc(xT_in_psum, 1)

            def router(f, p, k):
                pe.wait_ge(xnT_ready, p + 1)
                at_least(pe, gap_ready, f)
                for t in range(TPC):
                    last = nc.tensor.matmul(rpsum[:, t, :], xnT[:, k, t * P:(t + 1) * P], wr[:], start=True, stop=True)
                last.then_inc(logits_in_psum, 1)

            def expert_out(m, e):
                pe.wait_ge(act_ready, 2 * m + 2)
                at_least(pe, acc_done, m - 1)
                s = e % 2
                for t in range(TPC):
                    for j in range(2):
                        last = nc.tensor.matmul(ypsum[s][:, t, :], act[:, s, j, t * P:(t + 1) * P], w2[:, e, j, :],
                                                start=(j == 0), stop=(j == 1))
                last.then_inc(y_in_psum, 1)

            def out_projection(c):
                pe.wait_ge(attn_ready, c + 1)
                for t in range(TPC):
                    last = nc.tensor.matmul(tpsum[:, t * P:(t + 1) * P], attn[:, t * P:(t + 1) * P], wo[:], start=True, stop=True)
                last.then_inc(proj_in_psum, 1)

            def ffn_chunk(f, p, k, more, after_attention, first):
                for e in range(E):
                    m = E * f + e
                    for j in range(2):
                        a = 2 * m + j
                        at_least(pe, silu_done, a - 1)
                        nc.tensor.matmul(hid[2 * j], w1[:, e, F + j * P:F + (j + 1) * P], xnT[:, k, :],
                                         start=True, stop=True).then_inc(gate_in_psum, 1)
                        at_least(pe, act_ready, a - 1)
                        last = nc.tensor.matmul(hid[2 * j + 1], w1[:, e, j * P:(j + 1) * P], xnT[:, k, :],
                                                start=True, stop=True)
                        last.then_inc(value_in_psum, 1)
                    if e == E - 1:
                        pe.wait_ge(value_in_psum, 2 * m + 2)
                        pe.sem_inc(xnT_used, 1)
                    if not (first and e == 0):
                        expert_out(m - 1, (e - 1) % E)
                    if more and after_attention and e == 1:
                        out_projection(f - NCH + 1)
                    if more and e == 3:
                        x_transposes(p + 1, 1 - k)
                    if more and e == 5:
                        router(f + 1, p + 1, 1 - k)

            def ffn(f0, p0):
                rounds = NCH // CPB
                late = f0 > 0
                if late:
                    out_projection(0)
                x_transposes(p0, 0)
                router(f0, p0, 0)
                for u in range(CPB):
                    ffn_chunk(f0 + u, p0 + u, u, True, late, u == 0)
                with pe.Fori(1, rounds - 1) as r:
                    for u in range(CPB):
                        ffn_chunk(f0 + CPB * r + u, p0 + CPB * r + u, u, True, late, False)
                for u in range(CPB):
                    ffn_chunk(f0 + NCH - CPB + u, p0 + NCH - CPB + u, u, u < CPB - 1, late, False)
                expert_out(E * (f0 + NCH) - 1, E - 1)

            pe.wait_ge(w_loaded, 16 * 10)
            pe.wait_ge(consts_ready, 3)
            ffn(0, 0)

            pe.wait_ge(silu_done, 2 * E * NCH)
            pe.wait_ge(act_ready, 2 * E * NCH)
            pe.wait_ge(acc_done, E * NCH)

            def qkv_chunk(r, u):
                c = CPB * r + u
                x_transposes(NCH + c, u)
                pe.wait_ge(xnT_ready, NCH + c + 1)
                for w in range(2):
                    at_least(pe, qkv_read, 3 * c - 2 + w)
                    for i in range(2):
                        last = nc.tensor.matmul(hid[2 * w + i], wqkv[:, 2 * w + i, :], xnT[:, u, :], start=True, stop=True)
                    last.then_inc(qkv_in_psum, 1)
                at_least(pe, qkv_read, 3 * c)
                for t in range(TPC):
                    last = nc.tensor.matmul(ypsum[0][:, t, :], xnT[:, u, t * P:(t + 1) * P], wqkv[:, 4, :], start=True, stop=True)
                last.then_inc(qkv_in_psum, 1)
                pe.wait_ge(qkv_in_psum, 3 * c + 3)
                pe.sem_inc(xnT_used, 1)

            steps(pe, NCH, CPB, qkv_chunk)

            pe.wait_ge(qkv_read, 3 * NCH)
            pe.wait_ge(xnT_ready, 2 * NCH)

            def max_scores(r, u, t, half):
                n = QSLOTS * r + u
                if t == 0 and half == 0:
                    pe.wait_ge(head_loaded[u], 16 * (1 + PARTS) * (r + 1))
                at_least(pe, max_read, 2 * (KB * n + t) + half - 1)
                nc.tensor.matmul(maxps[half], Q[0:FILLED, u, t * P:(t + 1) * P],
                                 K[0:FILLED, u, half * CH:(half + 1) * CH], start=True, stop=True).then_inc(max_in_psum, 1)

            def max_transpose(r, u):
                n = QSLOTS * r + u
                pe.wait_ge(mparts_ready, n + 1)
                at_least(pe, ot_ready, n - 1)
                nc.tensor.transpose(mpsum[u % 2], mparts[:, u % 2, :, :].rearrange("p i t -> p (i t)"),
                                    identb[:]).then_inc(mT_in_psum, 1)

            def key_scores(r, u, kb, j):
                g = KB * (QSLOTS * r + u) + kb
                if kb == 0 and j == 0:
                    pe.wait_ge(mrow_loaded[u], 16 * (r + 1))
                if j == 0:
                    at_least(pe, probs_ready, g - 1)
                last = nc.tensor.matmul(score[kb % 2][:, j, :], K[0:ROWS, u, kb * P:(kb + 1) * P],
                                        Q[0:ROWS, u, j * CH:(j + 1) * CH], start=True, stop=True)
                if j == 1:
                    last.then_inc(scores_in_psum, 1)

            def weigh_values(r, u, kb):
                n = QSLOTS * r + u
                g = KB * n + kb
                pe.wait_ge(probs_ready, g + 1)
                if kb == 0:
                    pe.wait_ge(mrow_ready, n + 1)
                    pe.wait_ge(vh_ready, n + 1)
                for c in range(4):
                    last = nc.tensor.matmul(opsum[u % 2][32 * c:32 * c + VW, :], vh[:, u % 2, kb, :],
                                            probs[:, kb % PSLOTS, c * QG:(c + 1) * QG],
                                            start=(kb == 0), stop=(kb == KB - 1), skip_group_check=True)
                last.then_inc(probs_used, 1)

            for u in range(2):
                for t in range(KB):
                    for j in range(2):
                        max_scores(0, u, t, j)
            max_transpose(0, 0)

            def head(r, u, maxes=True, row=True, first=False):
                for kb in range(KB):
                    for j in range(2):
                        key_scores(r, u, kb, j)
                        if maxes:
                            max_scores(r + (u + 2) // QSLOTS, (u + 2) % QSLOTS, kb, j)
                    if kb >= 2:
                        weigh_values(r, u, kb - 2)
                    elif not first:
                        weigh_values(r + (u - 1) // QSLOTS, (u - 1) % QSLOTS, KB - 2 + kb)
                    if kb == 3 and row:
                        max_transpose(r + (u + 1) // QSLOTS, (u + 1) % QSLOTS)

            for u in range(QSLOTS):
                head(0, u, first=(u == 0))
            with pe.Fori(1, NH // QSLOTS - 1) as r:
                for u in range(QSLOTS):
                    head(r, u)
            for u in range(QSLOTS):
                head(NH // QSLOTS - 1, u, maxes=u < 2, row=u < 3)
            for kb in (KB - 2, KB - 1):
                weigh_values(NH // QSLOTS - 1, QSLOTS - 1, kb)
            pe.wait_ge(ot_ready, NH)
            pe.wait_ge(mrow_ready, NH)

            ffn(NCH, 2 * NCH)

        @block.vector
        def _(dve):
            norm, picks = Order(dve, norm_order), Order(dve, route_order)
            LN_OPS = 2 * TPC + 4 + 4 * NEWTON
            ROUTE_OPS = 3 * TPC + 4

            def tile_of(c, t):
                return bass.ds(c * TPC + t, 1)

            def layer_norm(p, c, k):
                norm.start(p * LN_OPS)
                alone(dve)
                for t in range(TPC):
                    norm.mark(nc.vector.bn_stats(stats[:, t, :], X[:, tile_of(c, t), :].rearrange("p a d -> p (a d)")))
                norm.wait()
                alone(dve)
                for t in range(TPC):
                    norm.mark(nc.vector.bn_aggr(mv[:, t, :], stats[:, t, :]))
                norm.wait()
                norm.then(nc.vector.tensor_scalar(var[:], mv[:, :, 1], EPS, None, ALU.add))
                norm.mark(nc.vector.tensor_scalar(half_var[:], var[:], -0.5, None, ALU.mult))
                norm.then(nc.vector.tensor_scalar(tmp[:].bitcast(I32), var[:].bitcast(I32), 1, None, ALU.arith_shift_right))
                norm.then(nc.vector.tensor_scalar(rstd[:].bitcast(I32), tmp[:].bitcast(I32), -1.0, float(0x5F3759DF),
                                                 ALU.mult, ALU.add))
                for _ in range(NEWTON):
                    norm.then(nc.vector.tensor_tensor(tmp[:], rstd[:], rstd[:], ALU.mult))
                    norm.then(nc.vector.tensor_tensor(tmp[:], tmp[:], half_var[:], ALU.mult))
                    norm.then(nc.vector.tensor_scalar(tmp[:], tmp[:], 1.5, None, ALU.add))
                    norm.then(nc.vector.tensor_tensor(rstd[:], rstd[:], tmp[:], ALU.mult))
                at_least(dve, xT_in_psum, p - 1)
                for t in range(TPC):
                    last = nc.vector.tensor_scalar(xn[:, k, t, :], X[:, tile_of(c, t), :].rearrange("p a d -> p (a d)"),
                                                   mv[:, t, 0:1], rstd[:, t:t + 1], ALU.subtract, ALU.mult)
                last.then_inc(xn_ready, 1)
                assert norm.k == LN_OPS, (norm.k, LN_OPS)

            def route(f, k):
                picks.start(f * ROUTE_OPS)
                dve.wait_ge(logits_in_psum, f + 1)
                picks.then(nc.vector.tensor_copy(logits[:], rpsum))
                alone(dve)
                for t in range(TPC):
                    picks.mark(nc.vector.max(top[:, t, :], logits[:, t, :]))
                picks.wait()
                nc.vector.tensor_tensor(gap[:], top[:, :, 0], top[:, :, 1], ALU.subtract).then_inc(gap_ready, 1)
                alone(dve)
                for t in range(TPC):
                    picks.mark(nc.vector.max_index(top_id[:, t, :], top[:, t, :], logits[:, t, :]))
                picks.wait()
                picks.mark(nc.vector.tensor_copy(top_idf[:], top_id[:, :, 0:2]))
                dve.wait_ge(tanh_ready, f + 1)
                picks.mark(nc.vector.tensor_scalar(wt[:, 0, :], tanh_gap[:], 0.25, 0.25, ALU.mult, ALU.add))
                picks.then(nc.vector.tensor_scalar(wt[:, 1, :], tanh_gap[:], -0.25, 0.25, ALU.mult, ALU.add))
                for t in range(TPC):
                    for i in range(2):
                        last = nc.vector.tensor_scalar(pick[:, i, t, :], expert_id[:], top_idf[:, t, i:i + 1],
                                                       wt[:, i, t:t + 1], ALU.is_equal, ALU.mult)
                    picks.mark(last)
                picks.wait()
                nc.vector.tensor_tensor(rw[:, k, :, :], pick[:, 0, :, :], pick[:, 1, :, :], ALU.add).then_inc(route_ready, 1)
                dve.wait_ge(route_ready, f + 1)
                assert picks.k == ROUTE_OPS, (picks.k, ROUTE_OPS)

            def gated(f, e):
                for j in range(2):
                    m = E * f + e
                    a = 2 * m + j
                    dve.wait_ge(value_in_psum, a + 1)
                    dve.wait_ge(silu_done, a + 1)
                    at_least(dve, y_in_psum, m - 1)
                    nc.vector.tensor_tensor(act[:, e % 2, j, :], hid[2 * j + 1], sg[:, j, :], ALU.mult).then_inc(act_ready, 1)

            def accumulate(m, e, c, k):
                dve.wait_ge(y_in_psum, m + 1)
                at_least(dve, acc_done, m)
                for t in range(TPC):
                    xt = X[:, tile_of(c, t), :].rearrange("p a d -> p (a d)")
                    last = nc.vector.scalar_tensor_tensor(out=xt, in0=ypsum[e % 2][:, t, :], scalar=rw[:, k, t, e:e + 1],
                                                          in1=xt, op0=ALU.mult, op1=ALU.add)
                last.then_inc(acc_done, 1)

            def add_attention(c):
                dve.wait_ge(att_loaded, 64 * (c + 1))
                nc.vector.reciprocal(rden[:], den[:]).then_inc(add_order, 1)
                dve.wait_ge(add_order, 2 * c + 1)
                at_least(dve, proj_in_psum, c)
                nc.vector.tensor_tensor(attn[:], att[:], rden[:], ALU.mult).then_inc(attn_ready, 1)
                dve.wait_ge(proj_in_psum, c + 1)
                xs = X[:, bass.ds(c * TPC, TPC), :].rearrange("p t d -> p (t d)")
                nc.vector.tensor_tensor(xs, tpsum, xs, ALU.add).then_inc(add_order, 1)
                dve.wait_ge(add_order, 2 * c + 2)

            def ffn_chunk(r, u, f0, p0, more, first):
                c = CPB * r + u
                f, p, k = f0 + c, p0 + c, u
                for e in range(E):
                    gated(f, e)
                    if e > 0:
                        accumulate(E * f + e - 1, e - 1, c, k)
                    elif not first:
                        accumulate(E * f - 1, E - 1, c - 1, 1 - k)
                    if more and e == 1:
                        if f0 > 0:
                            add_attention(c + 1)
                        layer_norm(p + 1, c + 1, 1 - k)
                    if more and e == 5:
                        route(f + 1, 1 - k)

            def ffn(f0, p0):
                rounds = NCH // CPB
                if f0 > 0:
                    add_attention(0)
                layer_norm(p0, 0, 0)
                route(f0, 0)
                for u in range(CPB):
                    ffn_chunk(0, u, f0, p0, True, u == 0)
                with dve.Fori(1, rounds - 1) as r:
                    for u in range(CPB):
                        ffn_chunk(r, u, f0, p0, True, False)
                for u in range(CPB):
                    ffn_chunk(rounds - 1, u, f0, p0, u < CPB - 1, False)
                accumulate(E * (f0 + NCH) - 1, E - 1, NCH - 1, 1)

            dve.wait_ge(x_loaded, 16 * NCH)
            dve.wait_ge(w_loaded, 16 * 10)
            dve.wait_ge(consts_ready, 3)
            ffn(0, 0)
            dve.wait_ge(acc_done, E * NCH)

            def qkv_chunk(r, u):
                c = CPB * r + u
                layer_norm(NCH + c, c, u)
                for w, sgn in ((0, None), (1, None)):
                    z = 2 * c + w
                    dve.wait_ge(qkv_in_psum, 3 * c + w + 1)
                    at_least(dve, rot_sum, z - 1)
                    at = slice(u * CH, (u + 1) * CH)
                    nc.vector.scalar_tensor_tensor(out=rot[:, w, 0, :], in0=hid[2 * w], scalar=bqk[:, 2 * w:2 * w + 1],
                                                   in1=cos[:, at], op0=ALU.add, op1=ALU.mult)
                    nc.vector.scalar_tensor_tensor(out=rot[:, w, 1, :], in0=hid[2 * w + 1],
                                                   scalar=bqk[:, 2 * w + 1:2 * w + 2],
                                                   in1=sin[:, at], op0=ALU.add, op1=ALU.mult).then_inc(rot_ready, 1)
                    dve.wait_ge(rot_ready, z + 1)
                    dve.sem_inc(qkv_read, 1)
                dve.wait_ge(qkv_in_psum, 3 * c + 3)
                for t in range(TPC):
                    v_at = V[:, bass.ds(r, 1), :, u * TPC + t, :].rearrange("p b h d -> p (b h) d")
                    last = nc.vector.tensor_tensor(v_at, ypsum[0][:, t, :].rearrange("p (h d) -> p h d", h=H),
                                                   bv[:].rearrange("p (h d) -> p h d", h=H), ALU.add)
                last.then_inc(qkv_read, 1)
                for t in range(TPC):
                    xt = X[:, tile_of(c, t), :].rearrange("p a d -> p (a d)")
                    last = nc.vector.tensor_tensor(xt, xt, bo[:], ALU.add)
                last.then_inc(bias_added, 1)

            steps(dve, NCH, CPB, qkv_chunk)
            dve.wait_ge(bias_added, NCH)

            def head_max(r, u):
                n = QSLOTS * r + u
                at_least(dve, mparts_ready, n - 1)
                for t in range(KB):
                    for j in range(2):
                        dve.wait_ge(max_in_psum, 2 * (KB * n + t) + j + 1)
                        nc.vector.tensor_reduce(mx[:, u % 2, j, t:t + 1], maxps[j], AX_X, ALU.max).then_inc(max_read, 1)
                dve.wait_ge(max_read, 2 * KB * (n + 1))
                nc.vector.tensor_tensor(mx[:, u % 2, 0, :], mx[:, u % 2, 0, :], mx[:, u % 2, 1, :], ALU.max)\
                    .then_inc(max_ready, 1)

            steps(dve, NH, QSLOTS, head_max)
            ffn(NCH, 2 * NCH)


_IN = ["x_in", "qkv_w", "qkv_b", "v_b", "out_w", "out_b", "wr_t", "w1_t", "w2_t", "cos_t", "sin_t"]


def rotary_tables():
    half = HD // 2
    freq = (np.float32(10000.0) ** (np.arange(0, HD, 2, dtype=np.float32) / np.float32(HD))).astype(np.float32)
    angle = (np.arange(T, dtype=np.float32)[None, :] * freq[:, None]).astype(np.float64)
    c, s = np.cos(angle).astype(np.float32), np.sin(angle).astype(np.float32)
    cos_t = np.tile(np.concatenate([c, c]), (H, 1))
    sin_t = np.tile(np.concatenate([-s, s]), (H, 1))
    assert cos_t.shape == (H * 2 * half, T)
    return np.ascontiguousarray(cos_t), np.ascontiguousarray(sin_t)


def kernel(L0_attn_x, L0_attn_qkv_w, L0_attn_qkv_b, L0_attn_out_w, L0_attn_out_b, L0_ffn_Wr, L0_ffn_W1, L0_ffn_W2):
    import concourse.bacc as bacc
    from concourse.bass_utils import run_bass_kernel_spmd

    dims = np.arange(D).reshape(H, HD)
    plain = np.concatenate([dims[:, ::2], dims[:, 1::2]], axis=1).ravel()
    swapped = np.concatenate([dims[:, 1::2], dims[:, ::2]], axis=1).ravel()
    columns = np.concatenate([plain, swapped, D + plain, D + swapped, 2 * D + np.arange(D)])
    w = np.asarray(L0_attn_qkv_w)
    b = np.asarray(L0_attn_qkv_b)
    cos_t, sin_t = rotary_tables()
    arrays = {
        "x_in": np.asarray(L0_attn_x).reshape(N, D),
        "qkv_w": w[:, columns].reshape(D, 5, D),
        "qkv_b": b[columns[:4 * D]].reshape(4, D).T,
        "v_b": b[2 * D:].reshape(1, D),
        "out_w": np.asarray(L0_attn_out_w),
        "out_b": np.asarray(L0_attn_out_b).reshape(1, D),
        "wr_t": np.asarray(L0_ffn_Wr).T,
        "w1_t": np.asarray(L0_ffn_W1).transpose(2, 0, 1),
        "w2_t": np.asarray(L0_ffn_W2).reshape(E, D, F // P, P).transpose(3, 0, 2, 1),
        "cos_t": cos_t,
        "sin_t": sin_t,
    }
    arrays = {name: np.ascontiguousarray(a) for name, a in arrays.items()}
    nc = bacc.Bacc("TRN2", target_bir_lowering=False, num_devices=1)
    args = [nc.dram_tensor(name, arrays[name].shape, F32, kind="ExternalInput").ap() for name in _IN]
    out = nc.dram_tensor("out", (N, D), F32, kind="ExternalOutput").ap()
    build(nc, *args, out)
    result = run_bass_kernel_spmd(nc, [arrays], core_ids=[0])
    return result.results[0]["out"].reshape(B, T, D)
```

```python
from contextlib import ExitStack

import numpy as np

import concourse.bass as bass
from concourse import mybir

F32 = mybir.dt.float32
BF16 = mybir.dt.bfloat16
F16 = mybir.dt.float16
U32 = mybir.dt.uint32
I32 = mybir.dt.int32
ALU = mybir.AluOpType
ACT = mybir.ActivationFunctionType
AX_X = mybir.AxisListType.X

P = 128
B, T, D = 4, 1024, 128
H, HD = 16, 8
E, F = 8, 256
N = B * T
EPS = 1e-5
BLK = 2 * F // P
X_SCALE = 2.0 ** 11
W_EXP = 14
TINY = 2.0 ** -99
SCALE = float(HD) ** -0.5
CH = 512
TPC = CH // P
NCH = N // CH
CPB = T // CH
NH = B * H
KB = T // P
PARTS = 3
STACK = PARTS * PARTS * HD
FILLED = 96
ROWS = FILLED + PARTS
QG = T // 4
VW = 32
QSLOTS = 4
PSLOTS = 4
HALVES = 2 * KB
W_OPS = 5
NEWTON = 3


def at_least(eng, sem, count):
    if isinstance(count, int) and count <= 0:
        return
    eng.wait_ge(sem, count)


class Order:

    def __init__(self, eng, sem):
        self.eng, self.sem, self.base, self.k = eng, sem, 0, 0

    def start(self, base):
        self.base, self.k = base, 0

    def mark(self, ins):
        self.k += 1
        ins.then_inc(self.sem, 1)

    def wait(self):
        self.eng.wait_ge(self.sem, self.base + self.k)

    def then(self, ins):
        self.mark(ins)
        self.wait()


def steps(eng, count, per, body):
    rounds = count // per
    for u in range(per):
        body(0, u)
    with eng.Fori(1, rounds - 1) as r:
        for u in range(per):
            body(r, u)
    for u in range(per):
        body(rounds - 1, u)


def build(nc, x_in, qkv_w, qkv_b, v_b, out_w, out_b, wr_t, w1_in, w2_t, cos_t, sin_t, out):
    q_stack = nc.dram_tensor("q_stack", (NH, PARTS, HD, T), BF16).ap()
    k_stack = nc.dram_tensor("k_stack", (NH, PARTS, HD, T), BF16).ap()
    o_parts = nc.dram_tensor("o_parts", (NH, P, QG), F32).ap()
    with ExitStack() as ctx:
        def sb(name, shape, dt=F32):
            return ctx.enter_context(nc.sbuf_tensor(name, shape, dt))

        def sem(name):
            return ctx.enter_context(nc.semaphore(name))

        w1_rows = sb("w1_rows", [P, E, BLK, D])
        w1_scaled = sb("w1_scaled", [P, 2, BLK, D])
        row_max = sb("row_max", [P, E, BLK])
        row_pow = sb("row_pow", [P, E, BLK])
        w_scale = sb("w_scale", [P, E, BLK])
        unscale = sb("unscale", [P, E, BLK])
        w1_hi = sb("w1_hi", [P, E, 2 * F], F16)
        w1_lo = sb("w1_lo", [P, E, 2 * F], F16)
        w2 = sb("w2", [P, E, F // P, D])
        wr = sb("wr", [P, E])
        wqkv = sb("wqkv", [P, 5, D])
        bqk = sb("bqk", [P, 4])
        bv = sb("bv", [P, D])
        wo = sb("wo", [P, D])
        bo = sb("bo", [P, D])
        cos = sb("cos", [P, T])
        sin = sb("sin", [P, T])
        ident = sb("ident", [P, P])
        identb = sb("identb", [P, P], BF16)
        expert_id = sb("expert_id", [P, E])
        X = sb("X", [P, N // P, D])
        V = sb("V", [P, B, H, KB, HD])
        stats = sb("stats", [P, TPC, 6])
        mv = sb("mv", [P, TPC, 2])
        var = sb("var", [P, TPC])
        half_var = sb("half_var", [P, TPC])
        rstd = sb("rstd", [P, TPC])
        tmp = sb("tmp", [P, TPC])
        xn = sb("xn", [P, 2, TPC, D])
        xnT = sb("xnT", [P, 2, CH])
        x_hi = sb("x_hi", [P, 2, CH], F16)
        x_lo = sb("x_lo", [P, 2, CH], F16)
        x2n = sb("x2n", [P, TPC, D])
        x2T = sb("x2T", [P, CH])
        logits = sb("logits", [P, TPC, E])
        top = sb("top", [P, TPC, 8])
        top_id = sb("top_id", [P, TPC, 8], U32)
        top_idf = sb("top_idf", [P, TPC, 2])
        gap = sb("gap", [P, TPC])
        tanh_gap = sb("tanh_gap", [P, TPC])
        wt = sb("wt", [P, 2, TPC])
        pick = sb("pick", [P, 2, TPC, E])
        rw = sb("rw", [P, 2, TPC, E])
        sg = sb("sg", [P, 2, CH])
        act = sb("act", [P, 2, 2, CH])
        rot = sb("rot", [P, 2, 2, CH])
        qf = sb("qf", [P, 2, CH])
        rest = sb("rest", [P, 2, CH])
        parts = sb("parts", [P, 2, PARTS, CH], BF16)
        Q = sb("Q", [P, QSLOTS, T], BF16)
        K = sb("K", [P, QSLOTS, T], BF16)
        probs = sb("probs", [P, PSLOTS, T])
        vh = sb("vh", [P, 2, KB, VW])
        mx = sb("mx", [P, 2, 2, KB])
        negm = sb("negm", [P, 2, KB])
        mparts = sb("mparts", [P, 2, PARTS, KB], BF16)
        mrow = sb("mrow", [PARTS * KB, 2, P], BF16)
        ot = sb("ot", [P, 2, QG])
        att = sb("att", [P, CH])
        den = sb("den", [P, CH])
        rden = sb("rden", [P, CH])
        attn = sb("attn", [P, CH])

        ps = ctx.enter_context(nc.psum_tensor("ps", [P, 8, 512], F32))
        hid = [ps[:, 0, :], ps[:, 1, :], ps[:, 2, :], ps[:, 3, :]]
        ypsum = [ps[:, 4 + s, :].rearrange("p (t c) -> p t c", t=TPC) for s in range(2)]
        tpsum = ps[:, 6, :]
        early_t = ps[:, 4, :]
        early_r = ps[:, 5, 0:TPC * E].rearrange("p (t e) -> p t e", t=TPC)
        mpsum_all = ps[:, 7, :]
        rpsum = ps[:, 7, 0:TPC * E].rearrange("p (t e) -> p t e", t=TPC)
        vpsum = ps[:, 7, :].rearrange("p (t h d) -> p t h d", t=TPC, h=H)
        score = [ps[:, 2 * s:2 * s + 2, :] for s in range(2)]
        maxps = [ps[:, 4 + s, :] for s in range(2)]
        opsum = [ps[:, 6 + s, 0:QG] for s in range(2)]
        mpsum = [ps[0:PARTS * KB, 6 + s, 0:P // 2].bitcast(BF16) for s in range(2)]

        expert_loaded = [sem(f"expert_loaded{e}") for e in range(E)]
        router_loaded = sem("router_loaded")
        w_loaded = sem("w_loaded")
        x_loaded = [sem("x_loaded0"), sem("x_loaded_rest")]
        consts_ready = sem("consts_ready")
        stacks_ready = sem("stacks_ready")
        pool_order = sem("pool_order")
        norm_order = sem("norm_order")
        route_order = sem("route_order")
        xn_ready = sem("xn_ready")
        xT_in_psum = sem("xT_in_psum")
        xnT_ready = sem("xnT_ready")
        x_hi_ready = sem("x_hi_ready")
        x_lo_ready = sem("x_lo_ready")
        w_order = sem("w_order")
        w_scaled = sem("w_scaled")
        wT_in_psum = sem("wT_in_psum")
        w_hi_ready = sem("w_hi_ready")
        w_lo_ready = sem("w_lo_ready")
        logits_in_psum = sem("logits_in_psum")
        gap_ready = sem("gap_ready")
        tanh_ready = sem("tanh_ready")
        route_ready = sem("route_ready")
        gate_in_psum = sem("gate_in_psum")
        value_in_psum = sem("value_in_psum")
        silu_done = sem("silu_done")
        act_ready = sem("act_ready")
        y_in_psum = sem("y_in_psum")
        acc_done = sem("acc_done")
        x2n_ready = sem("x2n_ready")
        x2T_in_psum = sem("x2T_in_psum")
        x2T_ready = sem("x2T_ready")
        qk_in_psum = sem("qk_in_psum")
        v_in_psum = sem("v_in_psum")
        v_ready = sem("v_ready")
        rot_ready = sem("rot_ready")
        rot_sum = sem("rot_sum")
        hi_ready = sem("hi_ready")
        rest_ready = sem("rest_ready")
        mid_ready = sem("mid_ready")
        lo_ready = sem("lo_ready")
        stored = [sem("q_stored"), sem("k_stored")]
        head_loaded = [sem(f"head_loaded{u}") for u in range(QSLOTS)]
        max_in_psum = sem("max_in_psum")
        max_read = sem("max_read")
        max_ready = sem("max_ready")
        mparts_ready = sem("mparts_ready")
        mT_in_psum = sem("mT_in_psum")
        mrow_ready = sem("mrow_ready")
        mrow_loaded = [sem(f"mrow_loaded{u}") for u in range(QSLOTS)]
        vh_ready = sem("vh_ready")
        scores_in_psum = sem("scores_in_psum")
        probs_ready = sem("probs_ready")
        probs_used = sem("probs_used")
        ot_ready = sem("ot_ready")
        ot_stored = [sem(f"ot_stored{s}") for s in range(2)]
        att_loaded = sem("att_loaded")
        attn_ready = sem("attn_ready")
        proj_in_psum = sem("proj_in_psum")
        waits_passed = sem("waits_passed")
        out_stored = sem("out_stored")
        add_order = sem("add_order")
        bias_added = sem("bias_added")

        def alone(eng):
            eng.sem_inc(waits_passed, 1)

        block = ctx.enter_context(nc.Block())

        @block.sync
        def _(sp):
            def load_x(c0, c1, done):
                sp.dma_start(X[:, TPC * c0:TPC * c1, :],
                             x_in[CH * c0:CH * c1, :].rearrange("(t p) d -> p t d", p=P)).then_inc(done, 16)

            load_x(0, 1, x_loaded[0])
            sp.dma_start(wr[:], wr_t).then_inc(router_loaded, 16)
            for e in range(E):
                sp.dma_start(w1_rows[:, e, :, :], w1_in[e].rearrange("(k p) c -> p k c", p=P)).then_inc(expert_loaded[e], 16)
                sp.dma_start(w2[:, e, :, :], w2_t[:, e, :, :]).then_inc(expert_loaded[e], 16)
                if e == 0:
                    load_x(1, NCH, x_loaded[1])
            for where, weight in ((wqkv[:], qkv_w), (bqk[:], qkv_b), (bv[:], v_b.to_broadcast((P, D))), (wo[:], out_w),
                                  (bo[:], out_b.to_broadcast((P, D))), (cos[:], cos_t), (sin[:], sin_t)):
                sp.dma_start(where, weight).then_inc(w_loaded, 16)

            def store_parts(r, u):
                for w, stack in ((0, q_stack), (1, k_stack)):
                    sp.wait_ge(lo_ready, 4 * r + 2 * u + w + 1)
                    for i in range(PARTS):
                        dst = stack[bass.ds(r * H, H), i, :, u * CH:(u + 1) * CH]
                        sp.dma_start(dst, parts[:, w, i, :]).then_inc(stored[w], 16)

            for u in range(CPB):
                store_parts(0, u)
            with sp.Fori(1, NCH // CPB - 1) as r:
                for u in range(CPB):
                    store_parts(r, u)
            store_parts(NCH // CPB - 1, 0)
            for w in range(2):
                sp.wait_ge(stored[w], 16 * PARTS * (NCH - 1))

            def load_head(r, u):
                n = QSLOTS * r + u
                at_least(sp, probs_used, KB * (n - QSLOTS + 1))
                q_part = q_stack[bass.ds(n, 1)].rearrange("n i d t -> n (i d) t").to_broadcast((PARTS, PARTS * HD, T))
                sp.dma_start(Q[0:STACK, u, :], q_part).then_inc(head_loaded[u], 16)
                for j in range(PARTS):
                    at = j * PARTS * HD
                    sp.dma_start(K[at:at + PARTS * HD, u, :],
                                 k_stack[bass.ds(n, 1), j, :, :].to_broadcast((PARTS, HD, T))).then_inc(head_loaded[u], 16)

            def load_mrow(r, u):
                n = QSLOTS * r + u
                sp.wait_ge(mrow_ready, n + 1)
                sp.dma_start(Q[FILLED:ROWS, u, :].rearrange("p (t c) -> p t c", t=KB),
                             mrow[:, u % 2, :]).then_inc(mrow_loaded[u], 16)

            def store_o(r, u):
                n = QSLOTS * r + u
                sp.wait_ge(ot_ready, n + 1)
                sp.dma_start(o_parts[bass.ds(n, 1)].rearrange("n p q -> (n p) q"), ot[:, u % 2, :]).then_inc(ot_stored[u % 2], 16)

            def later(r, u, by):
                return r + (u + by) // QSLOTS, (u + by) % QSLOTS

            sp.wait_ge(stacks_ready, 1)
            load_head(0, 0)
            load_head(0, 1)
            load_head(0, 2)
            store_parts(NCH // CPB - 1, 1)
            load_mrow(0, 0)
            for w in range(2):
                sp.wait_ge(stored[w], 16 * PARTS * NCH)

            def head(r, u, load=True, rows=True):
                if load:
                    load_head(*later(r, u, 3))
                if not (isinstance(r, int) and r == 0 and u == 0):
                    store_o(*later(r, u, -1))
                if rows:
                    load_mrow(*later(r, u, 1))

            def load_att(r, u):
                c = CPB * r + u
                at_least(sp, proj_in_psum, c)
                for g in range(2):
                    src = o_parts[bass.ds(r * H, H)]
                    at = 32 * (2 * u + g)
                    sp.dma_start(att[:, g * QG:(g + 1) * QG], src[:, at:at + HD, :]).then_inc(att_loaded, 16)
                    sp.dma_start(den[:, g * QG:(g + 1) * QG], src[:, at + HD:at + 2 * HD, :]).then_inc(att_loaded, 16)

            for u in range(QSLOTS):
                head(0, u)
            with sp.Fori(1, NH // QSLOTS - 1) as r:
                for u in range(QSLOTS):
                    head(r, u)
            last = NH // QSLOTS - 1
            for u in range(QSLOTS):
                head(last, u, load=u < 1, rows=u < 3)
                if u == 2:
                    for s in range(2):
                        sp.wait_ge(ot_stored[s], 16 * (NH // 2 - 1))
                    load_att(0, 0)
            store_o(last, QSLOTS - 1)
            for s in range(2):
                sp.wait_ge(ot_stored[s], 16 * NH // 2)

            def store_out(c):
                sp.wait_ge(acc_done, E * (NCH + c + 1))
                row = c * CH
                sp.dma_start(out[bass.ds(row, CH), :].rearrange("(t p) d -> p t d", p=P),
                             X[:, bass.ds(c * TPC, TPC), :]).then_inc(out_stored, 16)

            load_att(0, 1)

            def tail(r, u):
                load_att(*((r + 1, u)))
                store_out(CPB * r + u)

            with sp.Fori(0, NCH // CPB - 1) as r:
                for u in range(CPB):
                    tail(r, u)
            for u in range(CPB):
                store_out(NCH - CPB + u)
            sp.wait_ge(out_stored, 16 * NCH)

        @block.gpsimd
        def _(pool):
            seq = Order(pool, pool_order)
            seq.then(nc.gpsimd.memset(ident[:], 0.0))
            seq.then(nc.gpsimd.affine_select(out=ident[:], in_=ident[:], compare_op=ALU.not_equal, fill=1.0,
                                             base=0, pattern=[[-1, P]], channel_multiplier=1))
            for e in range(E):
                seq.then(nc.gpsimd.memset(expert_id[:, e:e + 1], float(e)))
            nc.gpsimd.tensor_copy(identb[:], ident[:]).then_inc(consts_ready, 1)
            seq.then(nc.gpsimd.memset(vh[:], 1.0))
            seq.then(nc.gpsimd.memset(Q[64:96, :, :], 0.0))
            seq.then(nc.gpsimd.memset(K[64:96, :, :], 0.0))
            nc.gpsimd.memset(K[96:P, :, :], 1.0).then_inc(stacks_ready, 1)
            pool.wait_ge(stacks_ready, 1)

            def split(r, u):
                for w in range(2):
                    z = 4 * r + 2 * u + w
                    pool.wait_ge(rot_ready, z + 1)
                    at_least(pool, mid_ready, z - 1)
                    nc.gpsimd.tensor_tensor(qf[:, w, :], rot[:, w, 0, :], rot[:, w, 1, :], ALU.add).then_inc(rot_sum, 1)
                    pool.wait_ge(rot_sum, z + 1)
                    pool.wait_ge(hi_ready, z + 1)
                    nc.gpsimd.tensor_tensor(rest[:, w, :], qf[:, w, :], parts[:, w, 0, :], ALU.subtract).then_inc(rest_ready, 1)
                    pool.wait_ge(rest_ready, z + 1)
                    pool.wait_ge(mid_ready, z + 1)
                    nc.gpsimd.tensor_tensor(parts[:, w, 2, :], rest[:, w, :], parts[:, w, 1, :], ALU.subtract).then_inc(lo_ready, 1)

            steps(pool, NCH, CPB, split)

            PER = 4
            order0 = seq.base + seq.k

            def max_parts(r, u):
                n = QSLOTS * r + u
                s = u % 2
                seq.start(PER * n + order0)
                pool.wait_ge(max_ready, n + 1)
                at_least(pool, mT_in_psum, n - 1)
                alone(pool)
                seq.then(nc.gpsimd.tensor_scalar(negm[:, 0, :], mx[:, s, 0, :], -1.0, None, ALU.mult))
                alone(pool)
                seq.then(nc.gpsimd.tensor_copy(mparts[:, s, 0, :], negm[:, 0, :]))
                seq.then(nc.gpsimd.tensor_tensor(negm[:, 1, :], negm[:, 0, :], mparts[:, s, 0, :], ALU.subtract))
                alone(pool)
                seq.then(nc.gpsimd.tensor_copy(mparts[:, s, 1, :], negm[:, 1, :]))
                nc.gpsimd.tensor_tensor(mparts[:, s, 2, :], negm[:, 1, :], mparts[:, s, 1, :], ALU.subtract).then_inc(mparts_ready, 1)

            def v_head(r, u):
                n = QSLOTS * r + u
                at_least(pool, probs_used, KB * (n - 1))
                alone(pool)
                nc.gpsimd.tensor_copy(vh[:, u % 2, :, 0:HD],
                                      V[:].rearrange("p b h k d -> p (b h) k d")[:, bass.ds(n, 1), :, :]
                                      .rearrange("p n k d -> p (n k) d")).then_inc(vh_ready, 1)

            pool.wait_ge(v_ready, NCH)
            pool.wait_ge(stacks_ready, 1)

            def head(r, u):
                v_head(r, u)
                max_parts(r, u)

            steps(pool, NH, QSLOTS, head)

        @block.scalar
        def _(sc):
            def xT_copy(p, k, bank=tpsum):
                sc.wait_ge(xT_in_psum, p + 1)
                at_least(sc, logits_in_psum, p - 1)
                nc.scalar.activation(xnT[:, k, :], bank, ACT.Copy).then_inc(xnT_ready, 1)
                at_least(sc, value_in_psum, 2 * E * (p - 1))
                nc.scalar.activation(x_hi[:, k, :], bank, ACT.Copy, scale=X_SCALE).then_inc(x_hi_ready, 1)

            def scale_rows(e):
                sc.wait_ge(w_order, W_OPS * (e + 1))
                sc.wait_ge(expert_loaded[e], 32)
                at_least(sc, wT_in_psum, e - 1)
                for k in range(BLK):
                    last = nc.scalar.activation(w1_scaled[:, e % 2, k, :], w1_rows[:, e, k, :], ACT.Copy,
                                                scale=w_scale[:, e, k:k + 1])
                last.then_inc(w_scaled, 1)

            def w_hi_part(e):
                sc.wait_ge(wT_in_psum, e + 1)
                nc.scalar.activation(w1_hi[:, e, :], mpsum_all, ACT.Copy).then_inc(w_hi_ready, 1)

            def x2T_copy(c):
                sc.wait_ge(x2T_in_psum, c + 1)
                at_least(sc, v_in_psum, c)
                nc.scalar.activation(x2T[:], tpsum, ACT.Copy).then_inc(x2T_ready, 1)

            def hi_part(c, w):
                sc.wait_ge(rot_sum, 2 * c + w + 1)
                at_least(sc, stored[w], 16 * PARTS * c)
                nc.scalar.activation(parts[:, w, 0, :], qf[:, w, :], ACT.Copy).then_inc(hi_ready, 1)

            def mid_part(c, w):
                sc.wait_ge(rest_ready, 2 * c + w + 1)
                nc.scalar.activation(parts[:, w, 1, :], rest[:, w, :], ACT.Copy).then_inc(mid_ready, 1)

            def tanh_of_gap(p):
                sc.wait_ge(gap_ready, p + 1)
                nc.scalar.activation(tanh_gap[:], gap[:], ACT.Tanh, scale=0.5).then_inc(tanh_ready, 1)

            def ffn_chunk(p, k, more, back, weights):
                for e in range(E):
                    if weights and e < E - 1:
                        scale_rows(e + 1)
                    for j in range(2):
                        a = 2 * (E * p + e) + j
                        sc.wait_ge(gate_in_psum, a + 1)
                        at_least(sc, act_ready, a - 1)
                        nc.scalar.activation(sg[:, j, :], hid[2 * j], ACT.Silu,
                                             scale=unscale[:, e, 2 + j:3 + j]).then_inc(silu_done, 1)
                    if weights and e < E - 1:
                        w_hi_part(e + 1)
                    if back is not None:
                        if e == 2:
                            x2T_copy(back)
                        if e == 4:
                            hi_part(back, 0)
                        if e == 5:
                            mid_part(back, 0)
                            hi_part(back, 1)
                        if e == 6:
                            mid_part(back, 1)
                    if more and e == 5:
                        xT_copy(p + 1, 1 - k)
                    if more and e == 7:
                        tanh_of_gap(p + 1)

            def ffn(p0, with_qkv):
                def chunk(c, u, more=True, back=True, weights=False):
                    ffn_chunk(p0 + c, u, more, c - 1 if back and with_qkv else None, weights)

                chunk(0, 0, back=False, weights=with_qkv)
                chunk(1, 1)
                with sc.Fori(1, NCH // CPB - 1) as r:
                    for u in range(CPB):
                        chunk(CPB * r + u, u)
                chunk(NCH - 2, 0)
                chunk(NCH - 1, 1, more=False)

            xT_copy(0, 0)
            scale_rows(0)
            w_hi_part(0)
            tanh_of_gap(0)
            ffn(0, True)
            x2T_copy(NCH - 1)
            for w in range(2):
                hi_part(NCH - 1, w)
                mid_part(NCH - 1, w)

            def mrow_copy(r, u):
                n = QSLOTS * r + u
                sc.wait_ge(mT_in_psum, n + 1)
                if not (isinstance(r, int) and r == 0 and u < 2):
                    back = (u - 2) % QSLOTS
                    sc.wait_ge(mrow_loaded[back], 16 * (r + (1 if u >= 2 else 0)))
                nc.scalar.activation(mrow[:, u % 2, :], mpsum[u % 2], ACT.Copy).then_inc(mrow_ready, 1)

            def o_copy(r, u):
                n = QSLOTS * r + u
                sc.wait_ge(probs_used, KB * (n + 1))
                if not (isinstance(r, int) and r == 0 and u < 2):
                    sc.wait_ge(ot_stored[u % 2], 16 * (2 * r + u // 2))
                nc.scalar.activation(ot[:, u % 2, :], opsum[u % 2], ACT.Copy).then_inc(ot_ready, 1)

            def head(r, u, more=True, first=False):
                n = QSLOTS * r + u
                for kb in range(KB):
                    g = KB * n + kb
                    sc.wait_ge(scores_in_psum, g + 1)
                    at_least(sc, probs_used, g - PSLOTS + 1)
                    nc.scalar.activation(probs[:, kb % PSLOTS, :], score[kb % 2].rearrange("p a b -> p (a b)"),
                                         ACT.Exp, scale=SCALE).then_inc(probs_ready, 1)
                    if kb == 2 and not first:
                        o_copy(r + (u - 1) // QSLOTS, (u - 1) % QSLOTS)
                    if kb == 5 and not more:
                        xT_copy(NCH, 0, early_t)
                    if kb == 4 and more:
                        mrow_copy(r + (u + 1) // QSLOTS, (u + 1) % QSLOTS)

            mrow_copy(0, 0)
            for u in range(QSLOTS):
                head(0, u, first=(u == 0))
            with sc.Fori(1, NH // QSLOTS - 1) as r:
                for u in range(QSLOTS):
                    head(r, u)
            for u in range(QSLOTS):
                head(NH // QSLOTS - 1, u, more=u < QSLOTS - 1)
            o_copy(NH // QSLOTS - 1, QSLOTS - 1)

            tanh_of_gap(NCH)
            ffn(NCH, False)

        @block.tensor
        def _(pe):
            def transposes(xs, bank=tpsum):
                for t in range(TPC):
                    last = nc.tensor.transpose(bank[:, t * P:(t + 1) * P], xs[:, t, :], ident[:])
                return last

            def x_transposes(p, k, rotated, bank=tpsum):
                pe.wait_ge(xn_ready, p + 1)
                at_least(pe, rot_ready, 2 * rotated)
                at_least(pe, x_lo_ready, p)
                transposes(xn[:, k, :, :], bank).then_inc(xT_in_psum, 1)

            def w_transposes(e):
                pe.wait_ge(w_scaled, e + 1)
                at_least(pe, w_lo_ready, e)
                if e > 0:
                    pe.wait_ge(gap_ready, 1)
                for k in range(BLK):
                    last = nc.tensor.transpose(mpsum_all[:, k * P:(k + 1) * P], w1_scaled[:, e % 2, k, :], ident[:])
                last.then_inc(wT_in_psum, 1)

            def x2_transposes(c):
                pe.wait_ge(x2n_ready, c + 1)
                at_least(pe, rot_ready, 2 * c)
                transposes(x2n).then_inc(x2T_in_psum, 1)

            def q_or_k(c, w):
                pe.wait_ge(x2T_ready, c + 1)
                if w:
                    pe.wait_ge(rot_ready, 2 * c + 1)
                else:
                    at_least(pe, route_ready, c)
                for i, bank in enumerate((mpsum_all, tpsum)):
                    last = nc.tensor.matmul(bank, wqkv[:, 2 * w + i, :], x2T[:], start=True, stop=True)
                last.then_inc(qk_in_psum, 1)

            def values(c):
                pe.wait_ge(rot_ready, 2 * c + 2)
                for t in range(TPC):
                    last = nc.tensor.matmul(mpsum_all[:, t * P:(t + 1) * P], x2T[:, t * P:(t + 1) * P], wqkv[:, 4, :],
                                            start=True, stop=True)
                last.then_inc(v_in_psum, 1)

            def router(p, k, valued, bank=rpsum):
                pe.wait_ge(xnT_ready, p + 1)
                at_least(pe, v_ready, valued)
                at_least(pe, gap_ready, p)
                if isinstance(p, int) and p < 2:
                    pe.wait_ge(w_lo_ready, 1 if p == 0 else E)
                for t in range(TPC):
                    last = nc.tensor.matmul(bank[:, t, :], xnT[:, k, t * P:(t + 1) * P], wr[:], start=True, stop=True)
                last.then_inc(logits_in_psum, 1)

            def expert_out(m, e):
                pe.wait_ge(act_ready, 2 * m + 2)
                at_least(pe, acc_done, m - 1)
                s = e % 2
                for t in range(TPC):
                    for j in range(2):
                        last = nc.tensor.matmul(ypsum[s][:, t, :], act[:, s, j, t * P:(t + 1) * P], w2[:, e, j, :],
                                                start=(j == 0), stop=(j == 1))
                last.then_inc(y_in_psum, 1)

            def out_projection(c, bank=tpsum):
                pe.wait_ge(attn_ready, c + 1)
                for t in range(TPC):
                    last = nc.tensor.matmul(bank[:, t * P:(t + 1) * P], attn[:, t * P:(t + 1) * P], wo[:], start=True, stop=True)
                last.then_inc(proj_in_psum, 1)

            def hidden(bank, e, at, k):
                for n, (w, x) in enumerate(((w1_hi, x_hi), (w1_hi, x_lo), (w1_lo, x_hi))):
                    last = nc.tensor.matmul(bank, w[:, e, at:at + P], x[:, k, :], start=(n == 0), stop=(n == 2))
                return last

            def ffn_chunk(p, k, first, more, back, proj, loads):
                done = 0 if back is None else back + 1
                for e in range(E):
                    m = E * p + e
                    if e == 0:
                        pe.wait_ge(x_lo_ready, p + 1)
                    if loads:
                        pe.wait_ge(expert_loaded[e], 32)
                        pe.wait_ge(w_lo_ready, e + 1)
                    for j in range(2):
                        a = 2 * m + j
                        at_least(pe, silu_done, a - 1)
                        hidden(hid[2 * j], e, F + j * P, k).then_inc(gate_in_psum, 1)
                        at_least(pe, act_ready, a - 1)
                        hidden(hid[2 * j + 1], e, j * P, k).then_inc(value_in_psum, 1)
                    if loads and e < E - 1:
                        w_transposes(e + 1)
                    if not (first and e == 0):
                        expert_out(m - 1, (e - 1) % E)
                    if proj is not None and e == 2:
                        out_projection(proj)
                    if back is not None:
                        if e == 2:
                            x2_transposes(back)
                        if e == 3:
                            q_or_k(back, 0)
                        if e == 4:
                            q_or_k(back, 1)
                        if e == 5:
                            values(back)
                    if more and e == 5:
                        x_transposes(p + 1, 1 - k, done)
                    if more and e == 6:
                        router(p + 1, 1 - k, done)

            def ffn(p0, attended):
                def chunk(c, u, first=False, more=True, loads=False):
                    back = None if attended or first else c - 1
                    ffn_chunk(p0 + c, u, first, more, back, c + 1 if attended and more else None, loads)

                if not attended:
                    x_transposes(p0, 0, 0)
                    w_transposes(0)
                    router(p0, 0, 0)
                chunk(0, 0, first=True, loads=not attended)
                if not attended:
                    pe.wait_ge(w_loaded, 16 * 7)
                chunk(1, 1)
                with pe.Fori(1, NCH // CPB - 1) as r:
                    for u in range(CPB):
                        chunk(CPB * r + u, u)
                chunk(NCH - 2, 0)
                chunk(NCH - 1, 1, more=False)
                expert_out(E * (p0 + NCH) - 1, E - 1)

            pe.wait_ge(router_loaded, 16)
            pe.wait_ge(consts_ready, 1)
            ffn(0, False)
            x2_transposes(NCH - 1)
            q_or_k(NCH - 1, 0)
            q_or_k(NCH - 1, 1)
            values(NCH - 1)

            pe.wait_ge(silu_done, 2 * E * NCH)
            pe.wait_ge(act_ready, 2 * E * NCH)
            pe.wait_ge(acc_done, E * NCH)
            pe.wait_ge(v_ready, NCH)

            def max_scores(r, u, t, half):
                n = QSLOTS * r + u
                if t == 0 and half == 0:
                    pe.wait_ge(head_loaded[u], 16 * (1 + PARTS) * (r + 1))
                at_least(pe, max_read, 2 * (KB * n + t) + half - 1)
                nc.tensor.matmul(maxps[half], Q[0:FILLED, u, t * P:(t + 1) * P],
                                 K[0:FILLED, u, half * CH:(half + 1) * CH], start=True, stop=True).then_inc(max_in_psum, 1)

            def max_transpose(r, u):
                n = QSLOTS * r + u
                pe.wait_ge(mparts_ready, n + 1)
                at_least(pe, ot_ready, n - 1)
                nc.tensor.transpose(mpsum[u % 2], mparts[:, u % 2, :, :].rearrange("p i t -> p (i t)"),
                                    identb[:]).then_inc(mT_in_psum, 1)

            def key_scores(r, u, kb, j):
                g = KB * (QSLOTS * r + u) + kb
                if kb == 0 and j == 0:
                    pe.wait_ge(mrow_loaded[u], 16 * (r + 1))
                if j == 0:
                    at_least(pe, probs_ready, g - 1)
                last = nc.tensor.matmul(score[kb % 2][:, j, :], K[0:ROWS, u, kb * P:(kb + 1) * P],
                                        Q[0:ROWS, u, j * CH:(j + 1) * CH], start=True, stop=True)
                if j == 1:
                    last.then_inc(scores_in_psum, 1)

            def weigh_values(r, u, kb):
                n = QSLOTS * r + u
                g = KB * n + kb
                pe.wait_ge(probs_ready, g + 1)
                if kb == 0:
                    pe.wait_ge(mrow_ready, n + 1)
                    pe.wait_ge(vh_ready, n + 1)
                for c in range(4):
                    last = nc.tensor.matmul(opsum[u % 2][32 * c:32 * c + VW, :], vh[:, u % 2, kb, :],
                                            probs[:, kb % PSLOTS, c * QG:(c + 1) * QG],
                                            start=(kb == 0), stop=(kb == KB - 1), skip_group_check=True)
                last.then_inc(probs_used, 1)

            for u in range(2):
                for t in range(KB):
                    for j in range(2):
                        max_scores(0, u, t, j)
            max_transpose(0, 0)

            def head(r, u, maxes=True, row=True, first=False, early=False):
                for kb in range(KB):
                    for j in range(2):
                        key_scores(r, u, kb, j)
                        if maxes:
                            max_scores(r + (u + 2) // QSLOTS, (u + 2) % QSLOTS, kb, j)
                    if kb >= 2:
                        weigh_values(r, u, kb - 2)
                    elif not first:
                        weigh_values(r + (u - 1) // QSLOTS, (u - 1) % QSLOTS, KB - 2 + kb)
                    if early and kb == 2:
                        pe.wait_ge(max_read, HALVES * NH)
                        out_projection(0, early_t)
                    if early and kb == 4:
                        x_transposes(NCH, 0, 0, early_t)
                    if early and kb == 6:
                        router(NCH, 0, 0, early_r)
                    if kb == 3 and row:
                        max_transpose(r + (u + 1) // QSLOTS, (u + 1) % QSLOTS)

            for u in range(QSLOTS):
                head(0, u, first=(u == 0))
            with pe.Fori(1, NH // QSLOTS - 1) as r:
                for u in range(QSLOTS):
                    head(r, u)
            for u in range(QSLOTS):
                head(NH // QSLOTS - 1, u, maxes=u < 2, row=u < 3, early=u == 3)
            for kb in (KB - 2, KB - 1):
                weigh_values(NH // QSLOTS - 1, QSLOTS - 1, kb)
            pe.wait_ge(ot_ready, NH)
            pe.wait_ge(mrow_ready, NH)
            pe.wait_ge(gap_ready, NCH + 1)

            ffn(NCH, True)

        @block.vector
        def _(dve):
            norm, picks, weights = Order(dve, norm_order), Order(dve, route_order), Order(dve, w_order)
            LN_OPS = 2 * TPC + 4 + 3 * NEWTON
            ROUTE_OPS = 3 * TPC + 4

            def tile_of(c, t):
                return bass.ds(c * TPC + t, 1)

            def flat(c, t):
                return X[:, tile_of(c, t), :].rearrange("p a d -> p (a d)")

            def norm_stats(i, c):
                norm.start(i * LN_OPS)
                alone(dve)
                for t in range(TPC):
                    norm.mark(nc.vector.bn_stats(stats[:, t, :], flat(c, t)))
                norm.wait()
                alone(dve)
                for t in range(TPC):
                    norm.mark(nc.vector.bn_aggr(mv[:, t, :], stats[:, t, :]))
                norm.wait()
                norm.then(nc.vector.tensor_scalar(var[:], mv[:, :, 1], EPS, None, ALU.add))
                norm.mark(nc.vector.tensor_scalar(half_var[:], var[:], -0.5, None, ALU.mult))
                norm.then(nc.vector.tensor_scalar(tmp[:].bitcast(I32), var[:].bitcast(I32), 1, None, ALU.arith_shift_right))
                norm.then(nc.vector.tensor_scalar(rstd[:].bitcast(I32), tmp[:].bitcast(I32), -1.0, float(0x5F3759DF),
                                                  ALU.mult, ALU.add))
                for _ in range(NEWTON):
                    norm.then(nc.vector.tensor_tensor(tmp[:], rstd[:], rstd[:], ALU.mult))
                    norm.then(nc.vector.tensor_tensor(tmp[:], tmp[:], half_var[:], ALU.mult))
                    norm.then(nc.vector.scalar_tensor_tensor(out=rstd[:], in0=tmp[:], scalar=1.5, in1=rstd[:],
                                                             op0=ALU.add, op1=ALU.mult))
                assert norm.k == LN_OPS, (norm.k, LN_OPS)

            def norm_apply(c, to, ready):
                for t in range(TPC):
                    last = nc.vector.tensor_scalar(to[:, t, :], flat(c, t), mv[:, t, 0:1], rstd[:, t:t + 1],
                                                   ALU.subtract, ALU.mult)
                last.then_inc(ready, 1)

            def x_lo_part(p, k, bank=tpsum):
                dve.wait_ge(x_hi_ready, p + 1)
                at_least(dve, value_in_psum, 2 * E * (p - 1))
                nc.vector.scalar_tensor_tensor(out=x_lo[:, k, :], in0=bank, scalar=X_SCALE, in1=x_hi[:, k, :],
                                               op0=ALU.mult, op1=ALU.subtract).then_inc(x_lo_ready, 1)

            def row_scales(e):
                weights.start(e * W_OPS)
                dve.wait_ge(expert_loaded[e], 32)
                weights.then(nc.vector.tensor_reduce(row_max[:, e, :], w1_rows[:, e, :, :], AX_X, ALU.max,
                                                     apply_absolute_value=True))
                weights.then(nc.vector.tensor_scalar(row_max[:, e, :], row_max[:, e, :], TINY, None, ALU.max))
                weights.then(nc.vector.tensor_scalar(row_pow[:, e, :].bitcast(I32), row_max[:, e, :].bitcast(I32),
                                                     0x7F800000, None, ALU.bitwise_and))
                weights.then(nc.vector.tensor_scalar(w_scale[:, e, :].bitcast(I32), row_pow[:, e, :].bitcast(I32), -1.0,
                                                     float((2 * 127 + W_EXP) << 23), ALU.mult, ALU.add))
                weights.then(nc.vector.tensor_scalar(unscale[:, e, :], row_pow[:, e, :], 2.0 ** -W_EXP / X_SCALE, None,
                                                     ALU.mult))
                assert weights.k == W_OPS, (weights.k, W_OPS)

            def w_lo_part(e):
                dve.wait_ge(w_hi_ready, e + 1)
                nc.vector.tensor_tensor(w1_lo[:, e, :], mpsum_all, w1_hi[:, e, :], ALU.subtract).then_inc(w_lo_ready, 1)

            def norm1(c, p, k):
                at_least(dve, xT_in_psum, p - 1)
                norm_apply(c, xn[:, k, :, :], xn_ready)

            def norm2(c):
                at_least(dve, x2T_in_psum, c)
                norm_apply(c, x2n, x2n_ready)

            def find_top(p, bank=rpsum):
                picks.start(p * ROUTE_OPS)
                dve.wait_ge(logits_in_psum, p + 1)
                picks.then(nc.vector.tensor_copy(logits[:], bank))
                alone(dve)
                for t in range(TPC):
                    picks.mark(nc.vector.max(top[:, t, :], logits[:, t, :]))
                picks.wait()
                nc.vector.tensor_tensor(gap[:], top[:, :, 0], top[:, :, 1], ALU.subtract).then_inc(gap_ready, 1)
                alone(dve)
                for t in range(TPC):
                    picks.mark(nc.vector.max_index(top_id[:, t, :], top[:, t, :], logits[:, t, :]))
                picks.wait()
                picks.mark(nc.vector.tensor_copy(top_idf[:], top_id[:, :, 0:2]))

            def route(p, k):
                picks.start(p * ROUTE_OPS)
                picks.k = 2 * TPC + 2
                dve.wait_ge(tanh_ready, p + 1)
                picks.mark(nc.vector.tensor_scalar(wt[:, 0, :], tanh_gap[:], 0.25, 0.25, ALU.mult, ALU.add))
                picks.then(nc.vector.tensor_scalar(wt[:, 1, :], tanh_gap[:], -0.25, 0.25, ALU.mult, ALU.add))
                for t in range(TPC):
                    for i in range(2):
                        last = nc.vector.tensor_scalar(pick[:, i, t, :], expert_id[:], top_idf[:, t, i:i + 1],
                                                       wt[:, i, t:t + 1], ALU.is_equal, ALU.mult)
                    picks.mark(last)
                picks.wait()
                assert picks.k == ROUTE_OPS, (picks.k, ROUTE_OPS)
                nc.vector.tensor_tensor(rw[:, k, :, :], pick[:, 0, :, :], pick[:, 1, :, :], ALU.add).then_inc(route_ready, 1)
                dve.wait_ge(route_ready, p + 1)

            def gated(f, e):
                for j in range(2):
                    m = E * f + e
                    a = 2 * m + j
                    dve.wait_ge(value_in_psum, a + 1)
                    dve.wait_ge(silu_done, a + 1)
                    at_least(dve, y_in_psum, m - 1)
                    nc.vector.scalar_tensor_tensor(out=act[:, e % 2, j, :], in0=hid[2 * j + 1],
                                                   scalar=unscale[:, e, j:j + 1], in1=sg[:, j, :],
                                                   op0=ALU.mult, op1=ALU.mult).then_inc(act_ready, 1)

            def accumulate(m, e, c, k):
                dve.wait_ge(y_in_psum, m + 1)
                at_least(dve, acc_done, m)
                for t in range(TPC):
                    xt = X[:, tile_of(c, t), :].rearrange("p a d -> p (a d)")
                    last = nc.vector.scalar_tensor_tensor(out=xt, in0=ypsum[e % 2][:, t, :], scalar=rw[:, k, t, e:e + 1],
                                                          in1=xt, op0=ALU.mult, op1=ALU.add)
                last.then_inc(acc_done, 1)

            def invert_denominator(c, half):
                at = slice(half * QG, (half + 1) * QG)
                if half == 0:
                    dve.wait_ge(att_loaded, 64 * (c + 1))
                nc.vector.reciprocal(rden[:, at], den[:, at]).then_inc(add_order, 1)

            def norm_attention(c):
                dve.wait_ge(add_order, 3 * c + 2)
                at_least(dve, proj_in_psum, c)
                nc.vector.tensor_tensor(attn[:], att[:], rden[:], ALU.mult).then_inc(attn_ready, 1)

            def add_attention(c, bank=tpsum):
                dve.wait_ge(proj_in_psum, c + 1)
                xs = X[:, bass.ds(c * TPC, TPC), :].rearrange("p t d -> p (t d)")
                nc.vector.tensor_tensor(xs, bank, xs, ALU.add).then_inc(add_order, 1)
                dve.wait_ge(add_order, 3 * c + 3)

            def rotate(c, u, w):
                z = 2 * c + w
                dve.wait_ge(qk_in_psum, z + 1)
                at_least(dve, rot_sum, z - 1)
                at = slice(u * CH, (u + 1) * CH)
                for i, (bank, table) in enumerate(((mpsum_all, cos), (tpsum, sin))):
                    last = nc.vector.scalar_tensor_tensor(out=rot[:, w, i, :], in0=bank,
                                                          scalar=bqk[:, 2 * w + i:2 * w + i + 1],
                                                          in1=table[:, at], op0=ALU.add, op1=ALU.mult)
                last.then_inc(rot_ready, 1)

            def keep_values(c, b, u):
                dve.wait_ge(v_in_psum, c + 1)
                for t in range(TPC):
                    v_at = V[:, bass.ds(b, 1), :, u * TPC + t, :].rearrange("p b h d -> p (b h) d")
                    last = nc.vector.tensor_tensor(v_at, vpsum[:, t, :, :], bv[:].rearrange("p (h d) -> p h d", h=H),
                                                   ALU.add)
                last.then_inc(v_ready, 1)

            def add_bias(c):
                for t in range(TPC):
                    last = nc.vector.tensor_tensor(flat(c, t), flat(c, t), bo[:], ALU.add)
                last.then_inc(bias_added, 1)

            def ffn_chunk(p0, r, u, first=False, more=True, route_now=True):
                c = CPB * r + u
                p, k = p0 + c, u
                attended = p0 > 0
                back = not attended and not first
                rb, ub = (r, 0) if u else (r - 1, 1)
                for e in range(E):
                    gated(p, e)
                    if first and not attended and e < E - 1:
                        w_lo_part(e + 1)
                        if e < E - 2:
                            row_scales(e + 2)
                    if e > 0:
                        accumulate(E * p + e - 1, e - 1, c, k)
                    elif not first:
                        accumulate(E * p - 1, E - 1, c - 1, 1 - k)
                    if e == 0:
                        if route_now:
                            route(p, k)
                        if attended and more:
                            invert_denominator(c + 1, 0)
                        if back:
                            dve.wait_ge(acc_done, E * p)
                            norm_stats(2 * c, c - 1)
                    if e == 1 and attended and more:
                        invert_denominator(c + 1, 1)
                        norm_attention(c + 1)
                    if e == 1 and back:
                        norm2(c - 1)
                    if e == 2 and more and not attended:
                        norm_stats(2 * c + 1, c + 1)
                    if e == 3 and more and not attended:
                        norm1(c + 1, p + 1, 1 - k)
                    if e == 3 and more and attended:
                        add_attention(c + 1)
                        norm_stats(2 * NCH + 1 + c, c + 1)
                    if e == 4 and more and attended:
                        norm1(c + 1, p + 1, 1 - k)
                    if e == 3 and back:
                        rotate(c - 1, ub, 0)
                    if e == 4 and back:
                        rotate(c - 1, ub, 1)
                        add_bias(c - 1)
                    if e == 5 and back:
                        keep_values(c - 1, rb, ub)
                    if e == 6 and more:
                        x_lo_part(p + 1, 1 - k)
                    if e == 7 and more:
                        find_top(p + 1)

            def ffn(p0):
                rounds = NCH // CPB
                ffn_chunk(p0, 0, 0, first=True, route_now=False)
                if p0 == 0:
                    dve.wait_ge(w_loaded, 16 * 7)
                ffn_chunk(p0, 0, 1)
                with dve.Fori(1, rounds - 1) as r:
                    for u in range(CPB):
                        ffn_chunk(p0, r, u)
                ffn_chunk(p0, rounds - 1, 0)
                ffn_chunk(p0, rounds - 1, 1, more=False)
                accumulate(E * (p0 + NCH) - 1, E - 1, NCH - 1, 1)

            dve.wait_ge(x_loaded[0], 16)
            dve.wait_ge(consts_ready, 1)
            norm_stats(0, 0)
            norm1(0, 0, 0)
            row_scales(0)
            x_lo_part(0, 0)
            w_lo_part(0)
            find_top(0)
            row_scales(1)
            route(0, 0)
            dve.wait_ge(x_loaded[1], 16)
            ffn(0)
            last_chunk = NCH - 1
            dve.wait_ge(acc_done, E * NCH)
            norm_stats(2 * NCH - 1, last_chunk)
            norm2(last_chunk)
            rotate(last_chunk, 1, 0)
            rotate(last_chunk, 1, 1)
            keep_values(last_chunk, B - 1, 1)
            add_bias(last_chunk)
            dve.wait_ge(bias_added, NCH)

            def head_max(r, u):
                n = QSLOTS * r + u
                at_least(dve, mparts_ready, n - 1)
                for t in range(KB):
                    for j in range(2):
                        dve.wait_ge(max_in_psum, 2 * (KB * n + t) + j + 1)
                        nc.vector.tensor_reduce(mx[:, u % 2, j, t:t + 1], maxps[j], AX_X, ALU.max).then_inc(max_read, 1)
                dve.wait_ge(max_read, 2 * KB * (n + 1))
                nc.vector.tensor_tensor(mx[:, u % 2, 0, :], mx[:, u % 2, 0, :], mx[:, u % 2, 1, :], ALU.max)\
                    .then_inc(max_ready, 1)

            steps(dve, NH, QSLOTS, head_max)
            invert_denominator(0, 0)
            invert_denominator(0, 1)
            norm_attention(0)
            add_attention(0, early_t)
            norm_stats(2 * NCH, 0)
            norm1(0, NCH, 0)
            x_lo_part(NCH, 0, early_t)
            find_top(NCH, early_r)
            route(NCH, 0)
            ffn(NCH)


_IN = ["x_in", "qkv_w", "qkv_b", "v_b", "out_w", "out_b", "wr_t", "w1_in", "w2_t", "cos_t", "sin_t"]


def rotary_tables():
    half = HD // 2
    freq = (np.float32(10000.0) ** (np.arange(0, HD, 2, dtype=np.float32) / np.float32(HD))).astype(np.float32)
    angle = (np.arange(T, dtype=np.float32)[None, :] * freq[:, None]).astype(np.float64)
    c, s = np.cos(angle).astype(np.float32), np.sin(angle).astype(np.float32)
    cos_t = np.tile(np.concatenate([c, c]), (H, 1))
    sin_t = np.tile(np.concatenate([-s, s]), (H, 1))
    assert cos_t.shape == (H * 2 * half, T)
    return np.ascontiguousarray(cos_t), np.ascontiguousarray(sin_t)


def kernel(L0_attn_x, L0_attn_qkv_w, L0_attn_qkv_b, L0_attn_out_w, L0_attn_out_b, L0_ffn_Wr, L0_ffn_W1, L0_ffn_W2):
    import concourse.bacc as bacc
    from concourse.bass_utils import run_bass_kernel_spmd

    dims = np.arange(D).reshape(H, HD)
    plain = np.concatenate([dims[:, ::2], dims[:, 1::2]], axis=1).ravel()
    swapped = np.concatenate([dims[:, 1::2], dims[:, ::2]], axis=1).ravel()
    columns = np.concatenate([plain, swapped, D + plain, D + swapped, 2 * D + np.arange(D)])
    w = np.asarray(L0_attn_qkv_w)
    b = np.asarray(L0_attn_qkv_b)
    cos_t, sin_t = rotary_tables()
    arrays = {
        "x_in": np.asarray(L0_attn_x).reshape(N, D),
        "qkv_w": w[:, columns].reshape(D, 5, D),
        "qkv_b": b[columns[:4 * D]].reshape(4, D).T,
        "v_b": b[2 * D:].reshape(1, D),
        "out_w": np.asarray(L0_attn_out_w),
        "out_b": np.asarray(L0_attn_out_b).reshape(1, D),
        "wr_t": np.asarray(L0_ffn_Wr).T,
        "w1_in": np.asarray(L0_ffn_W1),
        "w2_t": np.asarray(L0_ffn_W2).reshape(E, D, F // P, P).transpose(3, 0, 2, 1),
        "cos_t": cos_t,
        "sin_t": sin_t,
    }
    arrays = {name: np.ascontiguousarray(a) for name, a in arrays.items()}
    nc = bacc.Bacc("TRN2", target_bir_lowering=False, num_devices=1)
    args = [nc.dram_tensor(name, arrays[name].shape, F32, kind="ExternalInput").ap() for name in _IN]
    out = nc.dram_tensor("out", (N, D), F32, kind="ExternalOutput").ap()
    build(nc, *args, out)
    result = run_bass_kernel_spmd(nc, [arrays], core_ids=[0])
    return result.results[0]["out"].reshape(B, T, D)
```

```python
from contextlib import ExitStack

import numpy as np

import concourse.bass as bass
from concourse import mybir

F32 = mybir.dt.float32
BF16 = mybir.dt.bfloat16
F16 = mybir.dt.float16
U32 = mybir.dt.uint32
I32 = mybir.dt.int32
ALU = mybir.AluOpType
ACT = mybir.ActivationFunctionType
AX_X = mybir.AxisListType.X

P = 128
B, T, D = 4, 1024, 128
H, HD = 16, 8
E, F = 8, 256
N = B * T
EPS = 1e-5
BLK = 2 * F // P
X_SCALE = 2.0 ** 11
W_EXP = 14
TINY = 2.0 ** -99
SCALE = float(HD) ** -0.5
CH = 512
TPC = CH // P
NCH = N // CH
CPB = T // CH
NH = B * H
KB = T // P
PARTS = 3
STACK = PARTS * PARTS * HD
FILLED = 96
ROWS = FILLED + PARTS
PAIRS = KB // 2
VW = 32
PIECE = H * CH // P
QSLOTS = 4
PSLOTS = 8
HALVES = 2 * KB
MT_AT = 7
MAX_BANK = [(i + (i >= MT_AT) + (i == HALVES - 1)) % 3 for i in range(HALVES)]
MT_BANK = MT_AT % 3
W_OPS = 5
NEWTON = 3


def at_least(eng, sem, count):
    if isinstance(count, int) and count <= 0:
        return
    eng.wait_ge(sem, count)


class Order:

    def __init__(self, eng, sem):
        self.eng, self.sem, self.base, self.k = eng, sem, 0, 0

    def start(self, base):
        self.base, self.k = base, 0

    def mark(self, ins):
        self.k += 1
        ins.then_inc(self.sem, 1)

    def wait(self):
        self.eng.wait_ge(self.sem, self.base + self.k)

    def then(self, ins):
        self.mark(ins)
        self.wait()


def steps(eng, count, per, body, after={}):
    rounds = count // per
    for u in range(per):
        body(0, u)
    with eng.Fori(1, rounds - 1) as r:
        for u in range(per):
            body(r, u)
    for u in range(per):
        body(rounds - 1, u)
        after.get(per * (rounds - 1) + u, lambda: None)()


def build(nc, x_in, qkv_w, qkv_b, v_b, out_w, out_b, wr_t, w1_in, w2_t, cos_t, sin_t, out):
    q_stack = nc.dram_tensor("q_stack", (NH, PARTS, HD, T), BF16).ap()
    k_stack = nc.dram_tensor("k_stack", (NH, PARTS, HD, T), BF16).ap()
    rdens = nc.dram_tensor("rdens", (NCH, H, CH), F32).ap()
    o_parts = nc.dram_tensor("o_parts", (NH, P, CH), F32).ap()
    with ExitStack() as ctx:
        def sb(name, shape, dt=F32):
            return ctx.enter_context(nc.sbuf_tensor(name, shape, dt))

        def sem(name):
            return ctx.enter_context(nc.semaphore(name))

        w1_scaled = sb("w1_scaled", [P, 2, BLK, D])
        row_max = sb("row_max", [P, E, BLK])
        row_pow = sb("row_pow", [P, E, BLK])
        w_scale = sb("w_scale", [P, E, BLK])
        unscale = sb("unscale", [P, E, BLK])
        w1_hi = sb("w1_hi", [P, E, 2 * F], F16)
        w1_lo = sb("w1_lo", [P, E, 2 * F], F16)
        w2 = sb("w2", [P, E, F // P, D])
        wr = sb("wr", [P, E])
        wqkv = sb("wqkv", [P, 5, D])
        bqk = sb("bqk", [P, 4])
        bv = sb("bv", [P, D])
        wo = sb("wo", [P, D])
        bo = sb("bo", [P, D])
        cos = sb("cos", [P, T])
        sin = sb("sin", [P, T])
        ident = sb("ident", [P, P])
        identb = sb("identb", [P, P], BF16)
        expert_id = sb("expert_id", [P, E])
        X = sb("X", [P, N // P, D])
        V = sb("V", [P, B, H, KB, HD])
        stats = sb("stats", [P, 2, TPC, 6])
        mv = sb("mv", [P, 2, TPC, 2])
        var = sb("var", [P, 2, TPC])
        half_var = sb("half_var", [P, 2, TPC])
        rstd = sb("rstd", [P, 2, TPC])
        tmp = sb("tmp", [P, 2, TPC])
        xn = sb("xn", [P, 2, TPC, D])
        xnT = sb("xnT", [P, 2, CH])
        x_hi = sb("x_hi", [P, 2, CH], F16)
        x_lo = sb("x_lo", [P, 2, CH], F16)
        x2n = sb("x2n", [P, TPC, D])
        x2T = sb("x2T", [P, CH])
        logits = sb("logits", [P, TPC, E])
        top = sb("top", [P, TPC, 8])
        top_id = sb("top_id", [P, TPC, 8], U32)
        top_idf = sb("top_idf", [P, 2, TPC])
        gap = sb("gap", [P, TPC])
        tanh_gap = sb("tanh_gap", [P, TPC])
        wt = sb("wt", [P, 2, TPC])
        pick = sb("pick", [P, 2, TPC, E])
        rw = sb("rw", [P, 2, TPC, E])
        sg = sb("sg", [P, 2, CH])
        act = sb("act", [P, 2, 2, CH])
        rot = sb("rot", [P, 2, 2, CH])
        qf = sb("qf", [P, 2, CH])
        rest = sb("rest", [P, 2, CH])
        parts = sb("parts", [P, 2, PARTS, CH], BF16)
        Q = sb("Q", [P, QSLOTS, T], BF16)
        K = sb("K", [P, QSLOTS, T], BF16)
        probs = sb("probs", [P, PSLOTS, T])
        w1_rows = [probs[:, e // 2, e % 2 * 2 * F:(e % 2 + 1) * 2 * F].rearrange("p (k d) -> p k d", k=BLK)
                   for e in range(E)]
        vh = sb("vh", [P, 2, KB, VW])
        mx = sb("mx", [P, 2, 2, KB])
        negm = sb("negm", [P, 2, KB])
        mparts = sb("mparts", [P, 2, PARTS, KB], BF16)
        mrow = sb("mrow", [PARTS * KB, 2, P], BF16)
        ot = sb("ot", [P, 2, CH])
        att = sb("att", [P, 2, 2, CH])
        att_sum = sb("att_sum", [P, CH])
        den = sb("den", [P, 2, PIECE])
        den_sum = sb("den_sum", [P, PIECE])
        rden_thin = sb("rden_thin", [P, PIECE])
        rden = sb("rden", [P, 2, CH])
        attn = sb("attn", [P, CH])

        ps = ctx.enter_context(nc.psum_tensor("ps", [P, 8, 512], F32))
        hid = [ps[:, 0, :], ps[:, 1, :], ps[:, 2, :], ps[:, 3, :]]
        ypsum = [ps[:, 4 + s, :].rearrange("p (t c) -> p t c", t=TPC) for s in range(2)]
        tpsum = ps[:, 6, :]
        early_t = ps[:, 4, :]
        early_r = ps[:, 5, 0:TPC * E].rearrange("p (t e) -> p t e", t=TPC)
        mpsum_all = ps[:, 7, :]
        rpsum = ps[:, 7, 0:TPC * E].rearrange("p (t e) -> p t e", t=TPC)
        vpsum = ps[:, 7, :].rearrange("p (t h d) -> p t h d", t=TPC, h=H)
        score = [ps[:, 2 * s:2 * s + 2, :] for s in range(2)]
        maxps = [ps[:, 4 + s, :] for s in range(3)]
        mpsum = ps[0:PARTS * KB, 4 + MT_BANK, 0:P // 2].bitcast(BF16)
        opsum = ps[:, 7, :]

        expert_loaded = [sem(f"expert_loaded{e}") for e in range(E)]
        router_loaded = sem("router_loaded")
        w_loaded = sem("w_loaded")
        x_loaded = [sem("x_loaded0"), sem("x_loaded_rest")]
        consts_ready = sem("consts_ready")
        stacks_ready = sem("stacks_ready")
        pool_order = sem("pool_order")
        moments_order = sem("moments_order")
        rsqrt_order = sem("rsqrt_order")
        route_order = sem("route_order")
        xn_ready = sem("xn_ready")
        xT_in_psum = sem("xT_in_psum")
        xnT_ready = sem("xnT_ready")
        x_hi_ready = sem("x_hi_ready")
        x_lo_ready = sem("x_lo_ready")
        w_order = sem("w_order")
        w_scaled = sem("w_scaled")
        wT_in_psum = sem("wT_in_psum")
        w_hi_ready = sem("w_hi_ready")
        w_lo_ready = sem("w_lo_ready")
        logits_in_psum = sem("logits_in_psum")
        gap_ready = sem("gap_ready")
        tanh_ready = sem("tanh_ready")
        route_ready = sem("route_ready")
        gate_in_psum = sem("gate_in_psum")
        value_in_psum = sem("value_in_psum")
        silu_done = sem("silu_done")
        act_ready = sem("act_ready")
        y_in_psum = sem("y_in_psum")
        acc_done = sem("acc_done")
        x2n_ready = sem("x2n_ready")
        x2T_in_psum = sem("x2T_in_psum")
        x2T_ready = sem("x2T_ready")
        qk_in_psum = sem("qk_in_psum")
        v_in_psum = sem("v_in_psum")
        v_ready = sem("v_ready")
        rot_ready = sem("rot_ready")
        rot_sum = sem("rot_sum")
        hi_ready = sem("hi_ready")
        rest_ready = sem("rest_ready")
        mid_ready = sem("mid_ready")
        lo_ready = sem("lo_ready")
        stored = [sem("q_stored"), sem("k_stored")]
        head_loaded = [sem(f"head_loaded{u}") for u in range(QSLOTS)]
        max_in_psum = sem("max_in_psum")
        max_read = sem("max_read")
        max_ready = sem("max_ready")
        mparts_ready = sem("mparts_ready")
        mT_in_psum = sem("mT_in_psum")
        mrow_ready = sem("mrow_ready")
        mrow_loaded = [sem(f"mrow_loaded{u}") for u in range(QSLOTS)]
        vh_ready = sem("vh_ready")
        scores_in_psum = sem("scores_in_psum")
        probs_ready = sem("probs_ready")
        probs_used = sem("probs_used")
        ot_ready = sem("ot_ready")
        ot_stored = [sem(f"ot_stored{s}") for s in range(2)]
        att_loaded = [sem("att_loaded0"), sem("att_loaded1")]
        den_loaded = sem("den_loaded")
        den_summed = sem("den_summed")
        att_summed = sem("att_summed")
        den_inverted = sem("den_inverted")
        rden_stored = sem("rden_stored")
        attn_ready = sem("attn_ready")
        proj_in_psum = sem("proj_in_psum")
        waits_passed = sem("waits_passed")
        out_stored = sem("out_stored")
        add_order = sem("add_order")
        bias_added = sem("bias_added")

        def alone(eng):
            eng.sem_inc(waits_passed, 1)

        block = ctx.enter_context(nc.Block())

        @block.sync
        def _(sp):
            def load_x(c0, c1, done):
                sp.dma_start(X[:, TPC * c0:TPC * c1, :],
                             x_in[CH * c0:CH * c1, :].rearrange("(t p) d -> p t d", p=P)).then_inc(done, 16)

            load_x(0, 1, x_loaded[0])
            sp.dma_start(wr[:], wr_t).then_inc(router_loaded, 16)
            for e in range(E):
                sp.dma_start(w1_rows[e], w1_in[e].rearrange("(k p) c -> p k c", p=P)).then_inc(expert_loaded[e], 16)
                sp.dma_start(w2[:, e, :, :], w2_t[:, e, :, :]).then_inc(expert_loaded[e], 16)
                if e == 0:
                    load_x(1, NCH, x_loaded[1])
            for where, weight in ((wqkv[:], qkv_w), (bqk[:], qkv_b), (bv[:], v_b.to_broadcast((P, D))), (wo[:], out_w),
                                  (bo[:], out_b.to_broadcast((P, D))), (cos[:], cos_t), (sin[:], sin_t)):
                sp.dma_start(where, weight).then_inc(w_loaded, 16)

            def store_parts(r, u):
                for w, stack in ((0, q_stack), (1, k_stack)):
                    sp.wait_ge(lo_ready, 4 * r + 2 * u + w + 1)
                    for i in range(PARTS):
                        dst = stack[bass.ds(r * H, H), i, :, u * CH:(u + 1) * CH]
                        sp.dma_start(dst, parts[:, w, i, :]).then_inc(stored[w], 16)

            for u in range(CPB):
                store_parts(0, u)
            with sp.Fori(1, NCH // CPB - 1) as r:
                for u in range(CPB):
                    store_parts(r, u)
            store_parts(NCH // CPB - 1, 0)
            for w in range(2):
                sp.wait_ge(stored[w], 16 * PARTS * (NCH - 1))

            def load_head(r, u):
                n = QSLOTS * r + u
                at_least(sp, probs_used, PAIRS * (n - QSLOTS + 1))
                q_part = q_stack[bass.ds(n, 1)].rearrange("n i d t -> n (i d) t").to_broadcast((PARTS, PARTS * HD, T))
                sp.dma_start(Q[0:STACK, u, :], q_part).then_inc(head_loaded[u], 16)
                for j in range(PARTS):
                    at = j * PARTS * HD
                    sp.dma_start(K[at:at + PARTS * HD, u, :],
                                 k_stack[bass.ds(n, 1), j, :, :].to_broadcast((PARTS, HD, T))).then_inc(head_loaded[u], 16)

            def load_mrow(r, u):
                n = QSLOTS * r + u
                sp.wait_ge(mrow_ready, n + 1)
                sp.dma_start(Q[FILLED:ROWS, u, :].rearrange("p (t c) -> p t c", t=KB),
                             mrow[:, u % 2, :]).then_inc(mrow_loaded[u], 16)

            def store_o(r, u):
                n = QSLOTS * r + u
                sp.wait_ge(ot_ready, n + 1)
                sp.dma_start(o_parts[bass.ds(n, 1)].rearrange("n p q -> (n p) q"), ot[:, u % 2, :]).then_inc(ot_stored[u % 2], 16)

            def later(r, u, by):
                return r + (u + by) // QSLOTS, (u + by) % QSLOTS

            sp.wait_ge(stacks_ready, 1)
            load_head(0, 0)
            load_head(0, 1)
            load_head(0, 2)
            store_parts(NCH // CPB - 1, 1)
            load_mrow(0, 0)
            for w in range(2):
                sp.wait_ge(stored[w], 16 * PARTS * NCH)

            def head(r, u, load=True, rows=True):
                if load:
                    load_head(*later(r, u, 3))
                if not (isinstance(r, int) and r == 0 and u == 0):
                    store_o(*later(r, u, -1))
                if rows:
                    load_mrow(*later(r, u, 1))

            def load_den(r, u):
                c = CPB * r + u
                at_least(sp, den_inverted, c)
                for a in range(2):
                    src = o_parts[bass.ds(r * H, H), 32 * (2 * a + u) + HD, :].rearrange("h (s q) -> h s q", q=PIECE)
                    sp.dma_start(den[:, a, :], src).then_inc(den_loaded, 16)

            def load_att(r, u):
                c = CPB * r + u
                sp.wait_ge(den_inverted, c + 1)
                sp.dma_start(rdens[bass.ds(c, 1)].rearrange("c h (s q) -> (c h s) q", q=PIECE),
                             rden_thin[:]).then_inc(rden_stored, 16)
                at_least(sp, attn_ready, c - 1)
                alone(sp)
                sp.wait_ge(rden_stored, 16 * (c + 1))
                for a in range(2):
                    at = 32 * (2 * a + u)
                    sp.dma_start(att[:, u, a, :], o_parts[bass.ds(r * H, H), at:at + HD, :]).then_inc(att_loaded[u], 16)
                thin = rdens[bass.ds(c, 1)].rearrange("c h q -> (c h) q").unsqueeze(1).to_broadcast((H, HD, CH))
                sp.dma_start(rden[:, u, :], thin).then_inc(att_loaded[u], 16)

            for u in range(QSLOTS):
                head(0, u)
            with sp.Fori(1, NH // QSLOTS - 1) as r:
                for u in range(QSLOTS):
                    head(r, u)
            last = NH // QSLOTS - 1
            for s in range(2):
                sp.wait_ge(ot_stored[s], 16 * ((NH - QSLOTS - s) // 2))
            load_den(0, 0)
            for u in range(QSLOTS):
                head(last, u, load=u < 1, rows=u < 3)
                if u == 0:
                    load_att(0, 0)
                    load_den(0, 1)
            store_o(last, QSLOTS - 1)
            for s in range(2):
                sp.wait_ge(ot_stored[s], 16 * NH // 2)

            def store_out(c):
                sp.wait_ge(acc_done, E * (NCH + c + 1))
                row = c * CH
                sp.dma_start(out[bass.ds(row, CH), :].rearrange("(t p) d -> p t d", p=P),
                             X[:, bass.ds(c * TPC, TPC), :]).then_inc(out_stored, 16)

            load_att(0, 1)
            load_den(1, 0)

            def tail(r, u, att_ahead=True, den_ahead=True):
                if att_ahead:
                    load_att(r + 1, u)
                if den_ahead:
                    load_den(r + 1 + u, 1 - u)
                store_out(CPB * r + u)

            with sp.Fori(0, NCH // CPB - 2) as r:
                for u in range(CPB):
                    tail(r, u)
            tail(NCH // CPB - 2, 0)
            tail(NCH // CPB - 2, 1, den_ahead=False)
            for u in range(CPB):
                tail(NCH // CPB - 1, u, att_ahead=False, den_ahead=False)
            sp.wait_ge(out_stored, 16 * NCH)

        @block.gpsimd
        def _(pool):
            seq = Order(pool, pool_order)
            seq.then(nc.gpsimd.memset(ident[:], 0.0))
            seq.then(nc.gpsimd.affine_select(out=ident[:], in_=ident[:], compare_op=ALU.not_equal, fill=1.0,
                                             base=0, pattern=[[-1, P]], channel_multiplier=1))
            for e in range(E):
                seq.then(nc.gpsimd.memset(expert_id[:, e:e + 1], float(e)))
            nc.gpsimd.tensor_copy(identb[:], ident[:]).then_inc(consts_ready, 1)
            seq.then(nc.gpsimd.memset(vh[:], 1.0))
            seq.then(nc.gpsimd.memset(Q[64:96, :, :], 0.0))
            seq.then(nc.gpsimd.memset(K[64:96, :, :], 0.0))
            nc.gpsimd.memset(K[96:P, :, :], 1.0).then_inc(stacks_ready, 1)
            pool.wait_ge(stacks_ready, 1)

            def split(r, u):
                for w in range(2):
                    z = 4 * r + 2 * u + w
                    pool.wait_ge(rot_ready, z + 1)
                    at_least(pool, mid_ready, z - 1)
                    nc.gpsimd.tensor_tensor(qf[:, w, :], rot[:, w, 0, :], rot[:, w, 1, :], ALU.add).then_inc(rot_sum, 1)
                    pool.wait_ge(rot_sum, z + 1)
                    pool.wait_ge(hi_ready, z + 1)
                    nc.gpsimd.tensor_tensor(rest[:, w, :], qf[:, w, :], parts[:, w, 0, :], ALU.subtract).then_inc(rest_ready, 1)
                    pool.wait_ge(rest_ready, z + 1)
                    pool.wait_ge(mid_ready, z + 1)
                    nc.gpsimd.tensor_tensor(parts[:, w, 2, :], rest[:, w, :], parts[:, w, 1, :], ALU.subtract).then_inc(lo_ready, 1)

            steps(pool, NCH, CPB, split)

            PER = 4
            order0 = seq.base + seq.k

            def max_parts(r, u):
                n = QSLOTS * r + u
                s = u % 2
                seq.start(PER * n + order0)
                pool.wait_ge(max_ready, n + 1)
                at_least(pool, mT_in_psum, n - 1)
                alone(pool)
                seq.then(nc.gpsimd.tensor_scalar(negm[:, 0, :], mx[:, s, 0, :], -1.0, None, ALU.mult))
                alone(pool)
                seq.then(nc.gpsimd.tensor_copy(mparts[:, s, 0, :], negm[:, 0, :]))
                seq.then(nc.gpsimd.tensor_tensor(negm[:, 1, :], negm[:, 0, :], mparts[:, s, 0, :], ALU.subtract))
                alone(pool)
                seq.then(nc.gpsimd.tensor_copy(mparts[:, s, 1, :], negm[:, 1, :]))
                nc.gpsimd.tensor_tensor(mparts[:, s, 2, :], negm[:, 1, :], mparts[:, s, 1, :], ALU.subtract).then_inc(mparts_ready, 1)

            def v_head(r, u):
                n = QSLOTS * r + u
                at_least(pool, probs_used, PAIRS * (n - 1))
                alone(pool)
                nc.gpsimd.tensor_copy(vh[:, u % 2, :, 0:HD],
                                      V[:].rearrange("p b h k d -> p (b h) k d")[:, bass.ds(n, 1), :, :]
                                      .rearrange("p n k d -> p (n k) d")).then_inc(vh_ready, 1)

            pool.wait_ge(v_ready, NCH)
            pool.wait_ge(stacks_ready, 1)

            def head(r, u):
                max_parts(r, u)
                v_head(r, u)

            def sum_attention(r, u):
                c = CPB * r + u
                pool.wait_ge(att_loaded[u], 48 * (r + 1))
                at_least(pool, attn_ready, c)
                nc.gpsimd.tensor_tensor(att_sum[:], att[:, u, 0, :], att[:, u, 1, :], ALU.add).then_inc(att_summed, 1)

            steps(pool, NH, QSLOTS, head, {NH - 2: lambda: sum_attention(0, 0)})
            sum_attention(0, 1)
            with pool.Fori(1, NCH // CPB) as r:
                for u in range(CPB):
                    sum_attention(r, u)

        @block.scalar
        def _(sc):
            def xT_copy(p, k, bank=tpsum):
                sc.wait_ge(xT_in_psum, p + 1)
                at_least(sc, logits_in_psum, p - 1)
                nc.scalar.activation(xnT[:, k, :], bank, ACT.Copy).then_inc(xnT_ready, 1)
                at_least(sc, value_in_psum, 2 * E * (p - 1))
                nc.scalar.activation(x_hi[:, k, :], bank, ACT.Copy, scale=X_SCALE).then_inc(x_hi_ready, 1)

            def scale_rows(e):
                sc.wait_ge(w_order, W_OPS * (e + 1))
                sc.wait_ge(expert_loaded[e], 32)
                at_least(sc, wT_in_psum, e - 1)
                for k in range(BLK):
                    last = nc.scalar.activation(w1_scaled[:, e % 2, k, :], w1_rows[e][:, k, :], ACT.Copy,
                                                scale=w_scale[:, e, k:k + 1])
                last.then_inc(w_scaled, 1)

            def w_hi_part(e):
                sc.wait_ge(wT_in_psum, e + 1)
                nc.scalar.activation(w1_hi[:, e, :], mpsum_all, ACT.Copy).then_inc(w_hi_ready, 1)

            def x2T_copy(c):
                sc.wait_ge(x2T_in_psum, c + 1)
                at_least(sc, v_in_psum, c)
                nc.scalar.activation(x2T[:], tpsum, ACT.Copy).then_inc(x2T_ready, 1)

            def hi_part(c, w):
                sc.wait_ge(rot_sum, 2 * c + w + 1)
                at_least(sc, stored[w], 16 * PARTS * c)
                nc.scalar.activation(parts[:, w, 0, :], qf[:, w, :], ACT.Copy).then_inc(hi_ready, 1)

            def mid_part(c, w):
                sc.wait_ge(rest_ready, 2 * c + w + 1)
                nc.scalar.activation(parts[:, w, 1, :], rest[:, w, :], ACT.Copy).then_inc(mid_ready, 1)

            def tanh_of_gap(p):
                sc.wait_ge(gap_ready, p + 1)
                nc.scalar.activation(tanh_gap[:], gap[:], ACT.Tanh, scale=0.5).then_inc(tanh_ready, 1)

            def ffn_chunk(p, k, more, back, weights):
                for e in range(E):
                    if weights and e < E - 1:
                        scale_rows(e + 1)
                    for j in range(2):
                        a = 2 * (E * p + e) + j
                        sc.wait_ge(gate_in_psum, a + 1)
                        at_least(sc, act_ready, a - 1)
                        nc.scalar.activation(sg[:, j, :], hid[2 * j], ACT.Silu,
                                             scale=unscale[:, e, 2 + j:3 + j]).then_inc(silu_done, 1)
                    if weights and e < E - 1:
                        w_hi_part(e + 1)
                    if back is not None:
                        if e == 2:
                            x2T_copy(back)
                        if e == 4:
                            hi_part(back, 0)
                        if e == 5:
                            mid_part(back, 0)
                            hi_part(back, 1)
                        if e == 6:
                            mid_part(back, 1)
                    if more and e == 5:
                        xT_copy(p + 1, 1 - k)
                    if more and e == 7:
                        tanh_of_gap(p + 1)

            def ffn(p0, with_qkv):
                def chunk(c, u, more=True, back=True, weights=False):
                    ffn_chunk(p0 + c, u, more, c - 1 if back and with_qkv else None, weights)

                chunk(0, 0, back=False, weights=with_qkv)
                chunk(1, 1)
                with sc.Fori(1, NCH // CPB - 1) as r:
                    for u in range(CPB):
                        chunk(CPB * r + u, u)
                chunk(NCH - 2, 0)
                chunk(NCH - 1, 1, more=False)

            xT_copy(0, 0)
            scale_rows(0)
            w_hi_part(0)
            tanh_of_gap(0)
            ffn(0, True)
            x2T_copy(NCH - 1)
            for w in range(2):
                hi_part(NCH - 1, w)
                mid_part(NCH - 1, w)

            def mrow_copy(r, u):
                n = QSLOTS * r + u
                sc.wait_ge(mT_in_psum, n + 1)
                if not (isinstance(r, int) and r == 0 and u < 2):
                    back = (u - 2) % QSLOTS
                    sc.wait_ge(mrow_loaded[back], 16 * (r + (1 if u >= 2 else 0)))
                nc.scalar.activation(mrow[:, u % 2, :], mpsum, ACT.Copy).then_inc(mrow_ready, 1)

            def o_copy(r, u):
                n = QSLOTS * r + u
                sc.wait_ge(probs_used, PAIRS * (n + 1))
                if not (isinstance(r, int) and r == 0 and u < 2):
                    sc.wait_ge(ot_stored[u % 2], 16 * (2 * r + u // 2))
                nc.scalar.activation(ot[:, u % 2, :], opsum, ACT.Copy).then_inc(ot_ready, 1)

            def head(r, u, more=True, first=False):
                n = QSLOTS * r + u
                for kb in range(KB):
                    g = KB * n + kb
                    sc.wait_ge(scores_in_psum, g + 1)
                    if kb % 2 == 0:
                        at_least(sc, probs_used, PAIRS * (n - 1) + kb // 2 + 1)
                    nc.scalar.activation(probs[:, kb % PSLOTS, :], score[kb % 2].rearrange("p a b -> p (a b)"),
                                         ACT.Exp, scale=SCALE).then_inc(probs_ready, 1)
                    if kb == 1 and not first:
                        o_copy(r + (u - 1) // QSLOTS, (u - 1) % QSLOTS)
                    if kb == 2 and not more:
                        xT_copy(NCH, 0, early_t)
                    if kb == MT_AT // 2 - 1 and more:
                        mrow_copy(r + (u + 1) // QSLOTS, (u + 1) % QSLOTS)

            mrow_copy(0, 0)
            for u in range(QSLOTS):
                head(0, u, first=(u == 0))
            with sc.Fori(1, NH // QSLOTS - 1) as r:
                for u in range(QSLOTS):
                    head(r, u)
            for u in range(QSLOTS):
                head(NH // QSLOTS - 1, u, more=u < QSLOTS - 1)
            tanh_of_gap(NCH)
            o_copy(NH // QSLOTS - 1, QSLOTS - 1)

            ffn(NCH, False)

        @block.tensor
        def _(pe):
            def transposes(xs, bank=tpsum):
                for t in range(TPC):
                    last = nc.tensor.transpose(bank[:, t * P:(t + 1) * P], xs[:, t, :], ident[:])
                return last

            def x_transposes(p, k, rotated, bank=tpsum):
                pe.wait_ge(xn_ready, p + 1)
                at_least(pe, rot_ready, 2 * rotated)
                at_least(pe, x_lo_ready, p)
                transposes(xn[:, k, :, :], bank).then_inc(xT_in_psum, 1)

            def w_transposes(e):
                pe.wait_ge(w_scaled, e + 1)
                at_least(pe, w_lo_ready, e)
                if e > 0:
                    pe.wait_ge(gap_ready, 1)
                for k in range(BLK):
                    last = nc.tensor.transpose(mpsum_all[:, k * P:(k + 1) * P], w1_scaled[:, e % 2, k, :], ident[:])
                last.then_inc(wT_in_psum, 1)

            def x2_transposes(c):
                pe.wait_ge(x2n_ready, c + 1)
                at_least(pe, rot_ready, 2 * c)
                transposes(x2n).then_inc(x2T_in_psum, 1)

            def q_or_k(c, w):
                pe.wait_ge(x2T_ready, c + 1)
                if w:
                    pe.wait_ge(rot_ready, 2 * c + 1)
                else:
                    at_least(pe, route_ready, c)
                for i, bank in enumerate((mpsum_all, tpsum)):
                    last = nc.tensor.matmul(bank, wqkv[:, 2 * w + i, :], x2T[:], start=True, stop=True)
                last.then_inc(qk_in_psum, 1)

            def values(c):
                pe.wait_ge(rot_ready, 2 * c + 2)
                for t in range(TPC):
                    last = nc.tensor.matmul(mpsum_all[:, t * P:(t + 1) * P], x2T[:, t * P:(t + 1) * P], wqkv[:, 4, :],
                                            start=True, stop=True)
                last.then_inc(v_in_psum, 1)

            def router(p, k, valued, bank=rpsum):
                pe.wait_ge(xnT_ready, p + 1)
                at_least(pe, v_ready, valued)
                at_least(pe, gap_ready, p)
                if isinstance(p, int) and p < 2:
                    pe.wait_ge(w_lo_ready, 1 if p == 0 else E)
                for t in range(TPC):
                    last = nc.tensor.matmul(bank[:, t, :], xnT[:, k, t * P:(t + 1) * P], wr[:], start=True, stop=True)
                last.then_inc(logits_in_psum, 1)

            def expert_out(m, e):
                pe.wait_ge(act_ready, 2 * m + 2)
                at_least(pe, acc_done, m - 1)
                s = e % 2
                for t in range(TPC):
                    for j in range(2):
                        last = nc.tensor.matmul(ypsum[s][:, t, :], act[:, s, j, t * P:(t + 1) * P], w2[:, e, j, :],
                                                start=(j == 0), stop=(j == 1))
                last.then_inc(y_in_psum, 1)

            def out_projection(c, bank=tpsum):
                pe.wait_ge(attn_ready, c + 1)
                for t in range(TPC):
                    last = nc.tensor.matmul(bank[:, t * P:(t + 1) * P], attn[:, t * P:(t + 1) * P], wo[:], start=True, stop=True)
                last.then_inc(proj_in_psum, 1)

            def hidden(bank, e, at, k):
                for n, (w, x) in enumerate(((w1_hi, x_hi), (w1_hi, x_lo), (w1_lo, x_hi))):
                    last = nc.tensor.matmul(bank, w[:, e, at:at + P], x[:, k, :], start=(n == 0), stop=(n == 2))
                return last

            def ffn_chunk(p, k, first, more, back, proj, loads):
                done = 0 if back is None else back + 1
                for e in range(E):
                    m = E * p + e
                    if e == 0:
                        pe.wait_ge(x_lo_ready, p + 1)
                    if loads:
                        pe.wait_ge(expert_loaded[e], 32)
                        pe.wait_ge(w_lo_ready, e + 1)
                    for j in range(2):
                        a = 2 * m + j
                        at_least(pe, silu_done, a - 1)
                        hidden(hid[2 * j], e, F + j * P, k).then_inc(gate_in_psum, 1)
                        at_least(pe, act_ready, a - 1)
                        hidden(hid[2 * j + 1], e, j * P, k).then_inc(value_in_psum, 1)
                    if loads and e < E - 1:
                        w_transposes(e + 1)
                    if not (first and e == 0):
                        expert_out(m - 1, (e - 1) % E)
                    if proj is not None and e == 2:
                        out_projection(proj)
                    if back is not None:
                        if e == 2:
                            x2_transposes(back)
                        if e == 3:
                            q_or_k(back, 0)
                        if e == 4:
                            q_or_k(back, 1)
                        if e == 5:
                            values(back)
                    if more and e == 5:
                        x_transposes(p + 1, 1 - k, done)
                    if more and e == 6:
                        router(p + 1, 1 - k, done)

            def ffn(p0, attended):
                def chunk(c, u, first=False, more=True, loads=False):
                    back = None if attended or first else c - 1
                    ffn_chunk(p0 + c, u, first, more, back, c + 1 if attended and more else None, loads)

                if not attended:
                    x_transposes(p0, 0, 0)
                    w_transposes(0)
                    router(p0, 0, 0)
                chunk(0, 0, first=True, loads=not attended)
                if not attended:
                    pe.wait_ge(w_loaded, 16 * 7)
                chunk(1, 1)
                with pe.Fori(1, NCH // CPB - 1) as r:
                    for u in range(CPB):
                        chunk(CPB * r + u, u)
                chunk(NCH - 2, 0)
                chunk(NCH - 1, 1, more=False)
                expert_out(E * (p0 + NCH) - 1, E - 1)

            pe.wait_ge(router_loaded, 16)
            pe.wait_ge(consts_ready, 1)
            ffn(0, False)
            x2_transposes(NCH - 1)
            q_or_k(NCH - 1, 0)
            q_or_k(NCH - 1, 1)
            values(NCH - 1)

            pe.wait_ge(silu_done, 2 * E * NCH)
            pe.wait_ge(act_ready, 2 * E * NCH)
            pe.wait_ge(acc_done, E * NCH)
            pe.wait_ge(v_ready, NCH)

            def max_scores(r, u, t, half):
                i = 2 * t + half
                bank = MAX_BANK[i]
                before = max([b for b in range(i) if MAX_BANK[b] == bank], default=None)
                if before is None:
                    before = max(b for b in range(HALVES) if MAX_BANK[b] == bank) - HALVES
                n = QSLOTS * r + u
                if t == 0 and half == 0:
                    pe.wait_ge(head_loaded[u], 16 * (1 + PARTS) * (r + 1))
                at_least(pe, max_read, HALVES * n + before + 1)
                if bank == MT_BANK and before < MT_AT <= i:
                    at_least(pe, mrow_ready, n)
                nc.tensor.matmul(maxps[bank], Q[0:FILLED, u, t * P:(t + 1) * P],
                                 K[0:FILLED, u, half * CH:(half + 1) * CH], start=True, stop=True).then_inc(max_in_psum, 1)

            def max_transpose(r, u, maxes=True):
                n = QSLOTS * r + u
                pe.wait_ge(mparts_ready, n + 1)
                before = max(b for b in range(MT_AT if maxes else HALVES) if MAX_BANK[b] == MT_BANK)
                pe.wait_ge(max_read, HALVES * (n + 1 if maxes else n) + before + 1)
                nc.tensor.transpose(mpsum, mparts[:, u % 2, :, :].rearrange("p i t -> p (i t)"),
                                    identb[:]).then_inc(mT_in_psum, 1)

            def key_scores(r, u, kb, j):
                g = KB * (QSLOTS * r + u) + kb
                if kb == 0 and j == 0:
                    pe.wait_ge(mrow_loaded[u], 16 * (r + 1))
                if j == 0:
                    at_least(pe, probs_ready, g - 1)
                last = nc.tensor.matmul(score[kb % 2][:, j, :], K[0:ROWS, u, kb * P:(kb + 1) * P],
                                        Q[0:ROWS, u, j * CH:(j + 1) * CH], start=True, stop=True)
                if j == 1:
                    last.then_inc(scores_in_psum, 1)

            def weigh_values(r, u, pair):
                n = QSLOTS * r + u
                pe.wait_ge(probs_ready, KB * n + 2 * pair + 2)
                if pair == 0:
                    at_least(pe, ot_ready, n)
                    pe.wait_ge(vh_ready, n + 1)
                for c in range(4):
                    kb, j = 2 * pair + c // 2, c % 2
                    last = nc.tensor.matmul(opsum[32 * c:32 * c + VW, :], vh[:, u % 2, kb, :],
                                            probs[:, kb % PSLOTS, j * CH:(j + 1) * CH],
                                            start=(pair == 0), stop=(pair == PAIRS - 1), skip_group_check=True)
                last.then_inc(probs_used, 1)

            for u in range(2):
                for t in range(KB):
                    for j in range(2):
                        if u == 1 and 2 * t + j == MT_AT:
                            max_transpose(0, 0)
                        max_scores(0, u, t, j)

            def head(r, u, maxes=True, row=True, first=False, early=None):
                for kb in range(KB):
                    for j in range(2):
                        key_scores(r, u, kb, j)
                        if 2 * kb + j == MT_AT and row:
                            max_transpose(r + (u + 1) // QSLOTS, (u + 1) % QSLOTS, maxes)
                        if j == 1 and kb % 2 and kb >= 3:
                            weigh_values(r, u, kb // 2 - 1)
                        elif j == 1 and kb == 1 and not first:
                            weigh_values(r + (u - 1) // QSLOTS, (u - 1) % QSLOTS, PAIRS - 1)
                        if maxes:
                            max_scores(r + (u + 2) // QSLOTS, (u + 2) % QSLOTS, kb, j)
                    if early == 0 and kb == 2:
                        pe.wait_ge(max_read, HALVES * NH)
                        out_projection(0, early_t)
                    if early == 1 and kb == 1:
                        x_transposes(NCH, 0, 0, early_t)
                    if early == 1 and kb == 4:
                        router(NCH, 0, 0, early_r)

            for u in range(QSLOTS):
                head(0, u, first=(u == 0))
            with pe.Fori(1, NH // QSLOTS - 1) as r:
                for u in range(QSLOTS):
                    head(r, u)
            for u in range(QSLOTS):
                head(NH // QSLOTS - 1, u, maxes=u < 2, row=u < 3, early=u - 2)
            weigh_values(NH // QSLOTS - 1, QSLOTS - 1, PAIRS - 1)
            pe.wait_ge(ot_ready, NH)
            pe.wait_ge(mrow_ready, NH)
            pe.wait_ge(gap_ready, NCH + 1)

            ffn(NCH, True)

        @block.vector
        def _(dve):
            moment, rsqrt = Order(dve, moments_order), Order(dve, rsqrt_order)
            picks, weights = Order(dve, route_order), Order(dve, w_order)
            MOMENT_OPS = 2 * TPC
            RSQRT_OPS = 4 + 3 * NEWTON
            ROUTE_OPS = 2 * TPC + 6

            def tile_of(c, t):
                return bass.ds(c * TPC + t, 1)

            def flat(c, t):
                return X[:, tile_of(c, t), :].rearrange("p a d -> p (a d)")

            def moments(i, c, kind):
                moment.start(i * MOMENT_OPS)
                alone(dve)
                for t in range(TPC):
                    moment.mark(nc.vector.bn_stats(stats[:, kind, t, :], flat(c, t)))
                moment.wait()
                alone(dve)
                for t in range(TPC):
                    moment.mark(nc.vector.bn_aggr(mv[:, kind, t, :], stats[:, kind, t, :]))
                moment.wait()

            def inverse_std(i, first, last):
                rsqrt.start(i * RSQRT_OPS)
                v, h, y, w = (x[:, first:last + 1, :] for x in (var, half_var, rstd, tmp))
                rsqrt.then(nc.vector.tensor_scalar(v, mv[:, first:last + 1, :, 1], EPS, None, ALU.add))
                rsqrt.mark(nc.vector.tensor_scalar(h, v, -0.5, None, ALU.mult))
                rsqrt.then(nc.vector.tensor_scalar(w.bitcast(I32), v.bitcast(I32), 1, None, ALU.arith_shift_right))
                rsqrt.then(nc.vector.tensor_scalar(y.bitcast(I32), w.bitcast(I32), -1.0, float(0x5F3759DF),
                                                   ALU.mult, ALU.add))
                for _ in range(NEWTON):
                    rsqrt.then(nc.vector.tensor_tensor(w, y, y, ALU.mult))
                    rsqrt.then(nc.vector.tensor_tensor(w, w, h, ALU.mult))
                    rsqrt.then(nc.vector.scalar_tensor_tensor(out=y, in0=w, scalar=1.5, in1=y, op0=ALU.add, op1=ALU.mult))
                assert rsqrt.k == RSQRT_OPS, (rsqrt.k, RSQRT_OPS)

            def norm_apply(c, kind, to, ready):
                for t in range(TPC):
                    last = nc.vector.tensor_scalar(to[:, t, :], flat(c, t), mv[:, kind, t, 0:1], rstd[:, kind, t:t + 1],
                                                   ALU.subtract, ALU.mult)
                last.then_inc(ready, 1)

            def norm1(c, p, k):
                at_least(dve, xT_in_psum, p - 1)
                norm_apply(c, 0, xn[:, k, :, :], xn_ready)

            def norm2(c):
                at_least(dve, x2T_in_psum, c)
                norm_apply(c, 1, x2n, x2n_ready)

            def x_lo_part(p, k, bank=tpsum):
                dve.wait_ge(x_hi_ready, p + 1)
                at_least(dve, value_in_psum, 2 * E * (p - 1))
                nc.vector.scalar_tensor_tensor(out=x_lo[:, k, :], in0=bank, scalar=X_SCALE, in1=x_hi[:, k, :],
                                               op0=ALU.mult, op1=ALU.subtract).then_inc(x_lo_ready, 1)

            def row_scales(e):
                weights.start(e * W_OPS)
                dve.wait_ge(expert_loaded[e], 32)
                weights.then(nc.vector.tensor_reduce(row_max[:, e, :], w1_rows[e], AX_X, ALU.max,
                                                     apply_absolute_value=True))
                weights.then(nc.vector.tensor_scalar(row_max[:, e, :], row_max[:, e, :], TINY, None, ALU.max))
                weights.then(nc.vector.tensor_scalar(row_pow[:, e, :].bitcast(I32), row_max[:, e, :].bitcast(I32),
                                                     0x7F800000, None, ALU.bitwise_and))
                weights.then(nc.vector.tensor_scalar(w_scale[:, e, :].bitcast(I32), row_pow[:, e, :].bitcast(I32), -1.0,
                                                     float((2 * 127 + W_EXP) << 23), ALU.mult, ALU.add))
                weights.then(nc.vector.tensor_scalar(unscale[:, e, :], row_pow[:, e, :], 2.0 ** -W_EXP / X_SCALE, None,
                                                     ALU.mult))
                assert weights.k == W_OPS, (weights.k, W_OPS)

            def w_lo_part(e):
                dve.wait_ge(w_hi_ready, e + 1)
                nc.vector.tensor_tensor(w1_lo[:, e, :], mpsum_all, w1_hi[:, e, :], ALU.subtract).then_inc(w_lo_ready, 1)

            def find_top(p, bank=rpsum):
                picks.start(p * ROUTE_OPS)
                dve.wait_ge(logits_in_psum, p + 1)
                picks.then(nc.vector.tensor_copy(logits[:], bank))
                alone(dve)
                for t in range(TPC):
                    picks.mark(nc.vector.max(top[:, t, :], logits[:, t, :]))
                picks.wait()
                nc.vector.tensor_tensor(gap[:], top[:, :, 0], top[:, :, 1], ALU.subtract).then_inc(gap_ready, 1)
                alone(dve)
                for t in range(TPC):
                    picks.mark(nc.vector.max_index(top_id[:, t, :], top[:, t, :], logits[:, t, :]))
                picks.wait()
                picks.mark(nc.vector.tensor_copy(top_idf[:], top_id[:, :, 0:2].rearrange("p t i -> p i t")))

            def route(p, k):
                picks.start(p * ROUTE_OPS)
                picks.k = 2 * TPC + 2
                dve.wait_ge(tanh_ready, p + 1)
                picks.mark(nc.vector.tensor_scalar(wt[:, 0, :], tanh_gap[:], 0.25, 0.25, ALU.mult, ALU.add))
                picks.then(nc.vector.tensor_scalar(wt[:, 1, :], tanh_gap[:], -0.25, 0.25, ALU.mult, ALU.add))
                each = (P, 2, TPC, E)
                picks.then(nc.vector.tensor_tensor(pick[:], expert_id[:].unsqueeze(1).unsqueeze(1).to_broadcast(each),
                                                   top_idf[:].unsqueeze(3).to_broadcast(each), ALU.is_equal))
                picks.then(nc.vector.tensor_tensor(pick[:], pick[:], wt[:].unsqueeze(3).to_broadcast(each), ALU.mult))
                assert picks.k == ROUTE_OPS, (picks.k, ROUTE_OPS)
                nc.vector.tensor_tensor(rw[:, k, :, :], pick[:, 0, :, :], pick[:, 1, :, :], ALU.add).then_inc(route_ready, 1)
                dve.wait_ge(route_ready, p + 1)

            def gated(f, e):
                for j in range(2):
                    m = E * f + e
                    a = 2 * m + j
                    dve.wait_ge(value_in_psum, a + 1)
                    dve.wait_ge(silu_done, a + 1)
                    at_least(dve, y_in_psum, m - 1)
                    nc.vector.scalar_tensor_tensor(out=act[:, e % 2, j, :], in0=hid[2 * j + 1],
                                                   scalar=unscale[:, e, j:j + 1], in1=sg[:, j, :],
                                                   op0=ALU.mult, op1=ALU.mult).then_inc(act_ready, 1)

            def accumulate(m, e, c, k):
                dve.wait_ge(y_in_psum, m + 1)
                at_least(dve, acc_done, m)
                for t in range(TPC):
                    xt = X[:, tile_of(c, t), :].rearrange("p a d -> p (a d)")
                    last = nc.vector.scalar_tensor_tensor(out=xt, in0=ypsum[e % 2][:, t, :], scalar=rw[:, k, t, e:e + 1],
                                                          in1=xt, op0=ALU.mult, op1=ALU.add)
                last.then_inc(acc_done, 1)

            def invert_denominator(c):
                dve.wait_ge(den_loaded, 32 * (c + 1))
                nc.vector.tensor_tensor(den_sum[:], den[:, 0, :], den[:, 1, :], ALU.add).then_inc(den_summed, 1)
                dve.wait_ge(den_summed, c + 1)
                at_least(dve, rden_stored, 16 * c)
                alone(dve)
                nc.vector.reciprocal(rden_thin[:], den_sum[:]).then_inc(den_inverted, 1)

            def norm_attention(r, u):
                c = CPB * r + u
                dve.wait_ge(att_loaded[u], 48 * (r + 1))
                dve.wait_ge(att_summed, c + 1)
                at_least(dve, proj_in_psum, c)
                nc.vector.tensor_tensor(attn[:], att_sum[:], rden[:, u, :], ALU.mult).then_inc(attn_ready, 1)

            def add_attention(c, bank=tpsum):
                dve.wait_ge(proj_in_psum, c + 1)
                xs = X[:, bass.ds(c * TPC, TPC), :].rearrange("p t d -> p (t d)")
                nc.vector.tensor_tensor(xs, bank, xs, ALU.add).then_inc(add_order, 1)
                dve.wait_ge(add_order, c + 1)

            def rotate(c, u, w):
                z = 2 * c + w
                dve.wait_ge(qk_in_psum, z + 1)
                at_least(dve, rot_sum, z - 1)
                at = slice(u * CH, (u + 1) * CH)
                for i, (bank, table) in enumerate(((mpsum_all, cos), (tpsum, sin))):
                    last = nc.vector.scalar_tensor_tensor(out=rot[:, w, i, :], in0=bank,
                                                          scalar=bqk[:, 2 * w + i:2 * w + i + 1],
                                                          in1=table[:, at], op0=ALU.add, op1=ALU.mult)
                last.then_inc(rot_ready, 1)

            def keep_values(c, b, u):
                dve.wait_ge(v_in_psum, c + 1)
                for t in range(TPC):
                    v_at = V[:, bass.ds(b, 1), :, u * TPC + t, :].rearrange("p b h d -> p (b h) d")
                    last = nc.vector.tensor_tensor(v_at, vpsum[:, t, :, :], bv[:].rearrange("p (h d) -> p h d", h=H),
                                                   ALU.add)
                last.then_inc(v_ready, 1)

            def add_bias(c):
                for t in range(TPC):
                    last = nc.vector.tensor_tensor(flat(c, t), flat(c, t), bo[:], ALU.add)
                last.then_inc(bias_added, 1)

            def ffn_chunk(p0, r, u, first=False, more=True, route_now=True, ahead=True):
                c = CPB * r + u
                p, k = p0 + c, u
                attended = p0 > 0
                back = not attended and not first
                rb, ub = (r, 0) if u else (r - 1, 1)
                for e in range(E):
                    gated(p, e)
                    if first and not attended and e < E - 1:
                        w_lo_part(e + 1)
                        if e < E - 2:
                            row_scales(e + 2)
                    if attended and more and e == 5:
                        norm1(c + 1, p + 1, 1 - k)
                    if e > 0:
                        accumulate(E * p + e - 1, e - 1, c, k)
                    elif not first:
                        accumulate(E * p - 1, E - 1, c - 1, 1 - k)
                    if e == 0 and route_now:
                        route(p, k)
                    if not attended:
                        if e == 0 and first:
                            moments(1, 1, 0)
                        if e == 0 and back:
                            dve.wait_ge(acc_done, E * p)
                            moments(2 * c + 1 if more else 2 * c, c - 1, 1)
                        if e == 1:
                            inverse_std(c + 1, 0 if more else 1, 1 if back else 0)
                        if e == 1 and back:
                            norm2(c - 1)
                        if e == 2 and more:
                            norm1(c + 1, p + 1, 1 - k)
                        if e == 3 and back:
                            rotate(c - 1, ub, 0)
                        if e == 4 and back:
                            rotate(c - 1, ub, 1)
                            add_bias(c - 1)
                        if e == 5 and back:
                            keep_values(c - 1, rb, ub)
                    if attended and more:
                        if e == 1:
                            norm_attention(r + u, 1 - u)
                            if ahead:
                                invert_denominator(c + 2)
                        if e == 3:
                            add_attention(c + 1)
                            moments(2 * NCH + 1 + c, c + 1, 0)
                        if e == 4:
                            inverse_std(NCH + 3 + c, 0, 0)
                    if e == 6 and more:
                        x_lo_part(p + 1, 1 - k)
                        if not attended and ahead:
                            moments(2 * c + 2, c + 2, 0)
                    if e == 7 and more:
                        find_top(p + 1)

            def ffn(p0):
                rounds = NCH // CPB
                ffn_chunk(p0, 0, 0, first=True, route_now=False)
                if p0 == 0:
                    dve.wait_ge(w_loaded, 16 * 7)
                ffn_chunk(p0, 0, 1)
                with dve.Fori(1, rounds - 1) as r:
                    for u in range(CPB):
                        ffn_chunk(p0, r, u)
                ffn_chunk(p0, rounds - 1, 0, ahead=False)
                ffn_chunk(p0, rounds - 1, 1, more=False, ahead=False)
                accumulate(E * (p0 + NCH) - 1, E - 1, NCH - 1, 1)

            dve.wait_ge(x_loaded[0], 16)
            dve.wait_ge(consts_ready, 1)
            moments(0, 0, 0)
            inverse_std(0, 0, 0)
            norm1(0, 0, 0)
            row_scales(0)
            x_lo_part(0, 0)
            w_lo_part(0)
            find_top(0)
            row_scales(1)
            route(0, 0)
            dve.wait_ge(x_loaded[1], 16)
            ffn(0)
            last_chunk = NCH - 1
            dve.wait_ge(acc_done, E * NCH)
            moments(2 * NCH - 1, last_chunk, 1)
            inverse_std(NCH + 1, 1, 1)
            norm2(last_chunk)
            rotate(last_chunk, 1, 0)
            rotate(last_chunk, 1, 1)
            keep_values(last_chunk, B - 1, 1)
            add_bias(last_chunk)
            dve.wait_ge(bias_added, NCH)

            def head_max(r, u):
                n = QSLOTS * r + u
                at_least(dve, mparts_ready, n - 1)
                for t in range(KB):
                    for j in range(2):
                        dve.wait_ge(max_in_psum, 2 * (KB * n + t) + j + 1)
                        nc.vector.tensor_reduce(mx[:, u % 2, j, t:t + 1], maxps[MAX_BANK[2 * t + j]], AX_X, ALU.max).then_inc(max_read, 1)
                dve.wait_ge(max_read, 2 * KB * (n + 1))
                nc.vector.tensor_tensor(mx[:, u % 2, 0, :], mx[:, u % 2, 0, :], mx[:, u % 2, 1, :], ALU.max)\
                    .then_inc(max_ready, 1)

            steps(dve, NH, QSLOTS, head_max, {NH - 3: lambda: invert_denominator(0)})
            norm_attention(0, 0)
            add_attention(0, early_t)
            moments(2 * NCH, 0, 0)
            inverse_std(NCH + 2, 0, 0)
            invert_denominator(1)
            norm1(0, NCH, 0)
            x_lo_part(NCH, 0, early_t)
            find_top(NCH, early_r)
            route(NCH, 0)
            ffn(NCH)


_IN = ["x_in", "qkv_w", "qkv_b", "v_b", "out_w", "out_b", "wr_t", "w1_in", "w2_t", "cos_t", "sin_t"]


def rotary_tables():
    half = HD // 2
    freq = (np.float32(10000.0) ** (np.arange(0, HD, 2, dtype=np.float32) / np.float32(HD))).astype(np.float32)
    angle = (np.arange(T, dtype=np.float32)[None, :] * freq[:, None]).astype(np.float64)
    c, s = np.cos(angle).astype(np.float32), np.sin(angle).astype(np.float32)
    cos_t = np.tile(np.concatenate([c, c]), (H, 1))
    sin_t = np.tile(np.concatenate([-s, s]), (H, 1))
    assert cos_t.shape == (H * 2 * half, T)
    return np.ascontiguousarray(cos_t), np.ascontiguousarray(sin_t)


def kernel(L0_attn_x, L0_attn_qkv_w, L0_attn_qkv_b, L0_attn_out_w, L0_attn_out_b, L0_ffn_Wr, L0_ffn_W1, L0_ffn_W2):
    import concourse.bacc as bacc
    from concourse.bass_utils import run_bass_kernel_spmd

    dims = np.arange(D).reshape(H, HD)
    plain = np.concatenate([dims[:, ::2], dims[:, 1::2]], axis=1).ravel()
    swapped = np.concatenate([dims[:, 1::2], dims[:, ::2]], axis=1).ravel()
    columns = np.concatenate([plain, swapped, D + plain, D + swapped, 2 * D + np.arange(D)])
    w = np.asarray(L0_attn_qkv_w)
    b = np.asarray(L0_attn_qkv_b)
    cos_t, sin_t = rotary_tables()
    arrays = {
        "x_in": np.asarray(L0_attn_x).reshape(N, D),
        "qkv_w": w[:, columns].reshape(D, 5, D),
        "qkv_b": b[columns[:4 * D]].reshape(4, D).T,
        "v_b": b[2 * D:].reshape(1, D),
        "out_w": np.asarray(L0_attn_out_w),
        "out_b": np.asarray(L0_attn_out_b).reshape(1, D),
        "wr_t": np.asarray(L0_ffn_Wr).T,
        "w1_in": np.asarray(L0_ffn_W1),
        "w2_t": np.asarray(L0_ffn_W2).reshape(E, D, F // P, P).transpose(3, 0, 2, 1),
        "cos_t": cos_t,
        "sin_t": sin_t,
    }
    arrays = {name: np.ascontiguousarray(a) for name, a in arrays.items()}
    nc = bacc.Bacc("TRN2", target_bir_lowering=False, num_devices=1)
    args = [nc.dram_tensor(name, arrays[name].shape, F32, kind="ExternalInput").ap() for name in _IN]
    out = nc.dram_tensor("out", (N, D), F32, kind="ExternalOutput").ap()
    build(nc, *args, out)
    result = run_bass_kernel_spmd(nc, [arrays], core_ids=[0])
    return result.results[0]["out"].reshape(B, T, D)
```
